# Optimizing a Trainium2 kernel written in Bass

```python
import numpy as np
import jax
import jax.numpy as jnp

def _softmax(x, axis=-1):
    return jax.nn.softmax(x, axis=axis)

def _gelu(x):
    return jax.nn.gelu(x, approximate=True)

def _silu(x):
    return jax.nn.silu(x)

def _sigmoid(x):
    return jax.nn.sigmoid(x)

def _layernorm(x, axis=-1, eps=1e-05):
    m = jnp.mean(x, axis=axis, keepdims=True)
    v = jnp.var(x, axis=axis, keepdims=True)
    return (x - m) / jnp.sqrt(v + eps)

def _scatter_add(tgt, idx, src, axis=0):
    return tgt.at[idx].add(src)

def _segment_sum(src, seg, n):
    return jax.ops.segment_sum(src, seg, n)
kernel_name = 'mk_adj_ffn_d2_adj_r2_3367d3'

def setup_inputs(seed: int=0):
    np.random.seed(seed)
    _w = jnp.asarray

    def _rec_inputs():
        import jax
        import jax.numpy as jnp
        _gk = jax.random.key(seed)
        x = -0.0005207 + 1.001 * jax.random.normal(jax.random.fold_in(_gk, 1), (128, 128, 128), jnp.float32)
        _a = jax.random.bernoulli(jax.random.fold_in(_gk, 2), 0.125, (128, 128, 128))
        adj = _a.astype(jnp.int32)
        return (x, adj)
    x, adj = _rec_inputs()

    def _L0_gnn_setup():
        import jax, jax.numpy as jnp
        import numpy as np
        DIM = 128
        HEADS = 4
        B, N = (2, 2048)
        NEG = -1000000000.0
        EPS = 1e-05
        key = jax.random.key(seed)
        ks = jax.random.split(key, 12)
        s = 0.02
        inp = {'x': jax.random.normal(ks[0], (B, N, DIM), dtype=jnp.float32), 'adj': jax.random.randint(ks[1], (B, N, N), 0, 2, dtype=jnp.int32), 'Wq': jax.random.normal(ks[2], (DIM, DIM), dtype=jnp.float32) * s, 'bq': jnp.zeros((DIM,), jnp.float32), 'Wk': jax.random.normal(ks[3], (DIM, DIM), dtype=jnp.float32) * s, 'bk': jnp.zeros((DIM,), jnp.float32), 'Wv': jax.random.normal(ks[4], (DIM, DIM), dtype=jnp.float32) * s, 'bv': jnp.zeros((DIM,), jnp.float32), 'Wo': jax.random.normal(ks[5], (DIM, DIM), dtype=jnp.float32) * s, 'bo': jnp.zeros((DIM,), jnp.float32), 'gamma': jnp.ones((DIM,), jnp.float32), 'beta': jnp.zeros((DIM,), jnp.float32)}
        return inp
    _L0_gnn_all = _L0_gnn_setup()
    _L0_gnn_in = {k: v for k, v in _L0_gnn_all.items() if k in ('Wq', 'bq', 'Wk', 'bk', 'Wv', 'bv', 'Wo', 'bo', 'gamma', 'beta')}
    del _L0_gnn_all

    def _L0_ffn_setup():
        import jax, jax.numpy as jnp
        import numpy as np
        NUM_EXPERTS = 8
        TOP_K = 2
        B, S, D = (8, 4096, 128)

        def _moe(tokens, router_w, w1, b1, w2, b2):
            N = tokens.shape[0]
            E = router_w.shape[0]
            logits = tokens.astype(jnp.float32) @ router_w.astype(jnp.float32).T
            probs = jax.nn.softmax(logits, axis=-1)
            rw, re = jax.lax.top_k(probs, TOP_K)
            if TOP_K > 1:
                rw = rw / jnp.maximum(rw.sum(-1, keepdims=True), 1e-12)
            rw = rw.astype(tokens.dtype)
            combine = jnp.zeros((N, E), tokens.dtype).at[jnp.arange(N)[:, None], re].set(rw)
            out = tokens
            for e in range(E):
                h = jax.nn.gelu(tokens @ w1[e] + b1[e], approximate=False)
                y = h @ w2[e] + b2[e]
                out = out + combine[:, e:e + 1] * y
            return out
        key = jax.random.key(seed)
        ks = jax.random.split(key, 4)
        scale = 1.0 / np.sqrt(D).astype(np.float32)
        return {'input_embeddings': jax.random.normal(ks[0], (B, S, D), jnp.float32), 'router_w': jax.random.normal(ks[1], (NUM_EXPERTS, D), jnp.float32) * scale, 'w1': jax.random.normal(ks[2], (NUM_EXPERTS, D, D), jnp.float32) * scale, 'b1': jnp.zeros((NUM_EXPERTS, D), jnp.float32), 'w2': jax.random.normal(ks[3], (NUM_EXPERTS, D, D), jnp.float32) * scale, 'b2': jnp.zeros((NUM_EXPERTS, D), jnp.float32)}
    _L0_ffn_all = _L0_ffn_setup()
    _L0_ffn_in = {k: v for k, v in _L0_ffn_all.items() if k in ('router_w', 'w1', 'b1', 'w2', 'b2')}
    del _L0_ffn_all

    def _L1_gnn_setup():
        import jax, jax.numpy as jnp
        import numpy as np
        UNITS = 128
        NUM_HEADS = 8
        HEAD_DIM = UNITS // NUM_HEADS
        B, N = (8, 1024)
        key = jax.random.key(seed)
        ks = jax.random.split(key, 7)
        node_features = jax.random.normal(ks[0], (B, N, UNITS), dtype=jnp.float32)
        adjacency_matrix = jax.random.randint(ks[1], (B, N, N), 0, 2, dtype=jnp.int32)
        s = 1.0 / np.sqrt(UNITS)
        Wq = jax.random.normal(ks[2], (UNITS, UNITS), dtype=jnp.float32) * s
        Wk = jax.random.normal(ks[3], (UNITS, UNITS), dtype=jnp.float32) * s
        Wv = jax.random.normal(ks[4], (UNITS, UNITS), dtype=jnp.float32) * s
        Wo = jax.random.normal(ks[5], (UNITS, UNITS), dtype=jnp.float32) * s
        bo = jnp.zeros((UNITS,), dtype=jnp.float32)
        return {'node_features': node_features, 'adjacency_matrix': adjacency_matrix, 'Wq': Wq, 'Wk': Wk, 'Wv': Wv, 'Wo': Wo, 'bo': bo}
    _L1_gnn_all = _L1_gnn_setup()
    _L1_gnn_in = {k: v for k, v in _L1_gnn_all.items() if k in ('Wq', 'Wk', 'Wv', 'Wo', 'bo')}
    del _L1_gnn_all

    def _L1_ffn_setup():
        import jax, jax.numpy as jnp
        import numpy as np
        C = 128
        EPS = 1e-05
        N_ITERS = 30

        def _layernorm(x, w, bias):
            mu = jnp.mean(x, axis=-1, keepdims=True)
            var = jnp.mean(jnp.square(x - mu), axis=-1, keepdims=True)
            return (x - mu) * jax.lax.rsqrt(var + EPS) * w + bias
        key = jax.random.key(seed)
        kx, kw, kb, klw, klb = jax.random.split(key, 5)
        x = jax.random.normal(kx, (8, 1024, C), dtype=jnp.float32)
        bound = 1.0 / np.sqrt(C)
        W = jax.random.uniform(kw, (C, C), minval=-bound, maxval=bound, dtype=jnp.float32)
        b = jax.random.uniform(kb, (C,), minval=-bound, maxval=bound, dtype=jnp.float32)
        ln_w = jnp.ones((C,), dtype=jnp.float32)
        ln_b = jnp.zeros((C,), dtype=jnp.float32)
        return {'x': x, 'ln_w': ln_w, 'ln_b': ln_b, 'W': W, 'b': b}
    _L1_ffn_all = _L1_ffn_setup()
    _L1_ffn_in = {k: v for k, v in _L1_ffn_all.items() if k in ('ln_w', 'ln_b', 'W', 'b')}
    del _L1_ffn_all
    return {'x': x, 'adj': adj, 'L0_gnn_Wq': _L0_gnn_in['Wq'], 'L0_gnn_bq': _L0_gnn_in['bq'], 'L0_gnn_Wk': _L0_gnn_in['Wk'], 'L0_gnn_bk': _L0_gnn_in['bk'], 'L0_gnn_Wv': _L0_gnn_in['Wv'], 'L0_gnn_bv': _L0_gnn_in['bv'], 'L0_gnn_Wo': _L0_gnn_in['Wo'], 'L0_gnn_bo': _L0_gnn_in['bo'], 'L0_gnn_gamma': _L0_gnn_in['gamma'], 'L0_gnn_beta': _L0_gnn_in['beta'], 'L0_ffn_router_w': _L0_ffn_in['router_w'], 'L0_ffn_w1': _L0_ffn_in['w1'], 'L0_ffn_b1': _L0_ffn_in['b1'], 'L0_ffn_w2': _L0_ffn_in['w2'], 'L0_ffn_b2': _L0_ffn_in['b2'], 'L1_gnn_Wq': _L1_gnn_in['Wq'], 'L1_gnn_Wk': _L1_gnn_in['Wk'], 'L1_gnn_Wv': _L1_gnn_in['Wv'], 'L1_gnn_Wo': _L1_gnn_in['Wo'], 'L1_gnn_bo': _L1_gnn_in['bo'], 'L1_ffn_ln_w': _L1_ffn_in['ln_w'], 'L1_ffn_ln_b': _L1_ffn_in['ln_b'], 'L1_ffn_W': _L1_ffn_in['W'], 'L1_ffn_b': _L1_ffn_in['b']}

def reference(x, adj, L0_gnn_Wq, L0_gnn_bq, L0_gnn_Wk, L0_gnn_bk, L0_gnn_Wv, L0_gnn_bv, L0_gnn_Wo, L0_gnn_bo, L0_gnn_gamma, L0_gnn_beta, L0_ffn_router_w, L0_ffn_w1, L0_ffn_b1, L0_ffn_w2, L0_ffn_b2, L1_gnn_Wq, L1_gnn_Wk, L1_gnn_Wv, L1_gnn_Wo, L1_gnn_bo, L1_ffn_ln_w, L1_ffn_ln_b, L1_ffn_W, L1_ffn_b):
    import jax
    import jax.numpy as jnp

    def _L0_gnn_ref(x, adj, Wq, bq, Wk, bk, Wv, bv, Wo, bo, gamma, beta):
        import jax, jax.numpy as jnp
        import numpy as np
        DIM = 128
        HEADS = 4
        B, N = (2, 2048)
        NEG = -1000000000.0
        EPS = 1e-05
        Bx, Nx, C = x.shape
        H = HEADS
        D = C // H
        scale = D ** (-0.5)

        def proj(W, b):
            return (x @ W.T + b).reshape(Bx, Nx, H, D).transpose(0, 2, 1, 3)
        q = proj(Wq, bq)
        k = proj(Wk, bk)
        v = proj(Wv, bv)
        attn = jnp.einsum('bhnd,bhmd->bhnm', q, k) * scale
        attn = jnp.where(adj[:, None, :, :] == 0, NEG, attn)
        attn = jax.nn.softmax(attn, axis=-1)
        out = jnp.einsum('bhnm,bhmd->bhnd', attn, v)
        out = out.transpose(0, 2, 1, 3).reshape(Bx, Nx, C)
        out = out @ Wo.T + bo
        mu = jnp.mean(out, axis=-1, keepdims=True)
        var = jnp.var(out, axis=-1, keepdims=True)
        return (out - mu) * jax.lax.rsqrt(var + EPS) * gamma + beta

    def _L0_ffn_ref(input_embeddings, router_w, w1, b1, w2, b2):
        import jax, jax.numpy as jnp
        import numpy as np
        NUM_EXPERTS = 8
        TOP_K = 2
        B, S, D = (8, 4096, 128)

        def _moe(tokens, router_w, w1, b1, w2, b2):
            N = tokens.shape[0]
            E = router_w.shape[0]
            logits = tokens.astype(jnp.float32) @ router_w.astype(jnp.float32).T
            probs = jax.nn.softmax(logits, axis=-1)
            rw, re = jax.lax.top_k(probs, TOP_K)
            if TOP_K > 1:
                rw = rw / jnp.maximum(rw.sum(-1, keepdims=True), 1e-12)
            rw = rw.astype(tokens.dtype)
            combine = jnp.zeros((N, E), tokens.dtype).at[jnp.arange(N)[:, None], re].set(rw)
            out = tokens
            for e in range(E):
                h = jax.nn.gelu(tokens @ w1[e] + b1[e], approximate=False)
                y = h @ w2[e] + b2[e]
                out = out + combine[:, e:e + 1] * y
            return out
        b, s, d = input_embeddings.shape
        tokens = input_embeddings.reshape(b * s, d)
        return _moe(tokens, router_w, w1, b1, w2, b2).reshape(b, s, d)

    def _L1_gnn_ref(node_features, adjacency_matrix, Wq, Wk, Wv, Wo, bo):
        import jax, jax.numpy as jnp
        import numpy as np
        UNITS = 128
        NUM_HEADS = 8
        HEAD_DIM = UNITS // NUM_HEADS
        B, N = (8, 1024)
        b, n, _ = node_features.shape
        h, d = (NUM_HEADS, HEAD_DIM)
        q = (node_features @ Wq).reshape(b, n, h, d).transpose(0, 2, 1, 3)
        k = (node_features @ Wk).reshape(b, n, h, d).transpose(0, 2, 1, 3)
        v = (node_features @ Wv).reshape(b, n, h, d).transpose(0, 2, 1, 3)
        scores = jnp.einsum('bhqd,bhkd->bhqk', q, k) / jnp.sqrt(jnp.float32(d))
        mask = adjacency_matrix[:, None, :, :] > 0
        scores = jnp.where(mask, scores, jnp.float32(-1000000000.0))
        w = jax.nn.softmax(scores, axis=-1)
        ctx = jnp.einsum('bhqk,bhkd->bhqd', w, v)
        ctx = ctx.transpose(0, 2, 1, 3).reshape(b, n, h * d)
        return ctx @ Wo + bo

    def _L1_ffn_ref(x, ln_w, ln_b, W, b):
        import jax, jax.numpy as jnp
        import numpy as np
        C = 128
        EPS = 1e-05
        N_ITERS = 30

        def _layernorm(x, w, bias):
            mu = jnp.mean(x, axis=-1, keepdims=True)
            var = jnp.mean(jnp.square(x - mu), axis=-1, keepdims=True)
            return (x - mu) * jax.lax.rsqrt(var + EPS) * w + bias

        def step(h, _):
            h = h + 0.01 * jnp.tanh(h)
            h = h * jax.nn.sigmoid(h)
            h = _layernorm(h, ln_w, ln_b)
            h = jnp.einsum('bsc,dc->bsd', h, W) + b
            return (h, None)
        x, _ = jax.lax.scan(step, x, None, length=N_ITERS)
        return x
    x = x + _L0_gnn_ref(_layernorm(x, axis=-1), adj, L0_gnn_Wq, L0_gnn_bq, L0_gnn_Wk, L0_gnn_bk, L0_gnn_Wv, L0_gnn_bv, L0_gnn_Wo, L0_gnn_bo, L0_gnn_gamma, L0_gnn_beta)
    x = x + _L0_ffn_ref(_layernorm(x, axis=-1), L0_ffn_router_w, L0_ffn_w1, L0_ffn_b1, L0_ffn_w2, L0_ffn_b2)
    x = x + _L1_gnn_ref(_layernorm(x, axis=-1), adj, L1_gnn_Wq, L1_gnn_Wk, L1_gnn_Wv, L1_gnn_Wo, L1_gnn_bo)
    x = x + _L1_ffn_ref(_layernorm(x, axis=-1), L1_ffn_ln_w, L1_ffn_ln_b, L1_ffn_W, L1_ffn_b)
    return x

_drawn_inputs = setup_inputs


def setup_inputs(seed=0):
    import zlib

    import numpy as np

    out = dict(_drawn_inputs(seed))
    spreads = {'L0_gnn_bq': (0.0, 0.793),
     'L0_gnn_bk': (0.0, 0.8),
     'L0_gnn_bv': (0.0, 0.1),
     'L0_gnn_bo': (0.0, 0.1),
     'L0_gnn_gamma': (1.0, 0.2),
     'L0_gnn_beta': (0.0, 0.1),
     'L0_ffn_b1': (0.0, 0.284),
     'L0_ffn_b2': (0.0, 0.1),
     'L1_gnn_bo': (0.0, 0.1),
     'L1_ffn_ln_w': (1.0, 0.2),
     'L1_ffn_ln_b': (0.0, 0.1)}
    factors = {'L0_gnn_Wq': 4.209, 'L0_gnn_Wk': 3.947}
    for name, (base, spread) in spreads.items():
        noise = np.random.default_rng([zlib.crc32(name.encode()), seed]).standard_normal(out[name].shape)
        drawn = base * np.exp(spread * noise) if base else spread * noise
        out[name] = jnp.asarray(drawn.astype(out[name].dtype))
    for name, factor in factors.items():
        out[name] = (out[name] * factor).astype(out[name].dtype)
    return out
```

```python
import numpy as np
from contextlib import ExitStack
from concourse import bass, mybir

F32 = mybir.dt.float32
BF16 = mybir.dt.bfloat16
I32 = mybir.dt.int32
ALU = mybir.AluOpType
ACT = mybir.ActivationFunctionType
AX = mybir.AxisListType
P = 128
EPS = 1e-5
MASKED = -2.0 ** 100


def graph_attention(nc, env, tag, x_sb, adj, weights, heads, transposed, normed, masked_op, N_GRAPHS=128, x_in=None):
    D = P // heads
    HU = 4
    UG = heads // HU
    QG = 4
    NU = QG * UG
    QUADS = N_GRAPHS // QG
    TOTAL = QUADS * NU
    SCALE = float(np.float32(D) ** np.float32(-0.5))
    VW = D + 1
    QUAD = QG * P
    KEY_SLOTS = NU // 2

    with ExitStack() as ctx:
        sb = lambda n, s, d=F32: ctx.enter_context(nc.sbuf_tensor(tag + n, s, d))
        pb = lambda n, s, d=F32: ctx.enter_context(nc.psum_tensor(tag + n, s, d))
        sem = lambda n: ctx.enter_context(nc.semaphore(tag + n))
        ident, ident_bf, minus_half = env["ident"], env["ident_bf"], env["minus_half"]

        w_raw = sb("w_raw", [P, 4, P])
        w_q, w_k, w_v, w_o = (sb(f"w_{x}", [P, P]) for x in "qkvo")
        head_mask = sb("head_mask", [P, heads])
        cols_in = sb("cols_in", [P, 3])
        bv_bc = sb("bv_bc", [P, P])
        out_bias = sb("out_bias", [P, P])
        gamma = sb("gamma", [P, P])
        beta = sb("beta", [P, P])
        adj_in = sb("adj_in", [P, 2, QG, P], I32)
        mask = sb("mask", [P, 2, QG, P], BF16)
        stats = sb("stats", [P, QG // 2, 2, 3])
        var = sb("var", [P, QG])
        rstd = sb("rstd", [P, QG])
        xn = sb("xn", [P, QG, P])
        xn_t = sb("xn_t", [P, 2, QUAD])
        q_t = sb("q_t", [P, 2, QUAD])
        k_heads = sb("k_heads", [P, 2, QG, heads, P])
        v_ones = sb("v_ones", [P, 2, QG, heads, VW])
        neg_max = sb("neg_max", [P, 2, HU])
        row_max = sb("row_max", [P, 2, HU])
        prob = sb("prob", [P, 2, HU, P])
        prob_t = sb("prob_t", [P, 2, HU, P])
        rden = sb("rden", [P, HU])
        context = sb("context", [P, 2, P])
        context_t = sb("context_t", [P, 2, P])
        if normed:
            proj = sb("proj", [P, QG, P])
            stats_o = sb("stats_o", [P, QG // 2, 2, 3])
            var_o = sb("var_o", [P, QG])
            rstd_o = sb("rstd_o", [P, QG])
            proj_n = sb("proj_n", [P, QG, P])

        p_s = pb("p_s", [P, 2, HU, P])
        p_pt = pb("p_pt", [P, HU, P])
        p_pv = pb("p_pv", [P, HU, VW])
        p_ct = pb("p_ct", [P, P])
        p_o = pb("p_o", [P, QG, P])
        p_a = pb("p_a", [P, QUAD])
        p_b = pb("p_b", [P, QUAD])

        s_w = sem("weights_loaded")
        s_wt = sem("weight_transposed")
        s_prep = sem("prep_chain")
        s_hm = sem("head_mask_chain")
        s_x = sem("x_loaded") if x_in is not None else None
        s_adj = [sem(f"adj_loaded_{i}") for i in range(2)]
        s_mask = sem("mask_ready")
        s_ln = sem("ln_chain")
        s_var = sem("var_ready")
        s_rstd = sem("rstd_ready")
        s_xn = sem("xn_ready")
        s_xt = sem("xn_transposed")
        s_xtc = sem("xn_t_ready")
        s_qmm = sem("q_product")
        s_kmm = sem("k_product")
        s_vmm = sem("v_product")
        s_q = sem("q_ready")
        s_k = sem("k_ready")
        s_v = sem("v_ready")
        s_s = sem("scores_ready")
        s_max = sem("row_max_ready")
        s_neg = sem("neg_max_ready")
        s_exp = sem("prob_ready")
        s_tr = sem("prob_transposed")
        s_ptc = sem("prob_t_ready")
        s_pv = sem("context_product")
        s_rden = sem("rden_ready")
        s_norm = sem("context_ready")
        s_ct = sem("context_transposed")
        s_ctc = sem("context_t_ready")
        s_o = sem("projection_ready")
        s_fin = sem("projection_taken")
        s_fln = sem("out_ln_chain")
        s_fvar = sem("out_var_ready")
        s_frstd = sem("out_rstd_ready")
        s_fn = sem("out_normed")
        s_fp = sem("out_pool_chain")
        s_done = sem("x_updated")

        Wq, Wk, Wv, Wo, bq, bk, bv, bo, g_in, b_in = weights

        def live(q, limit):
            return not isinstance(q, int) or 0 <= q < limit

        def wait(eng, s, value):
            if not isinstance(value, int) or value > 0:
                eng.wait_ge(s, value)

        def quads(eng, body):
            for j in (-1, 0, 1):
                body(j, 0)
                body(j, 1)
            with eng.Fori(2, QUADS // 2 - 1) as j:
                body(j, 0)
                body(j, 1)
            for j in (QUADS // 2 - 1, QUADS // 2):
                body(j, 0)
                body(j, 1)

        def unit(k, u, ahead):
            return k + (u + ahead) // NU, (u + ahead) % NU

        adj_v = adj.rearrange("g n m -> n g m")
        row = lambda v: v.rearrange("(a c) -> a c", a=1).broadcast_to([P, P])
        col = lambda v: v.rearrange("(c a) -> c a", a=1)
        quad_row = lambda t: t[:].rearrange("p (a c) -> p a c", a=1).broadcast_to([P, QG, P])
        n_weights = 16 * (10 if normed else 5)
        n_prep = 6 if normed else 4

        with nc.Block() as block:
            @block.sync
            def _(sp):
                if x_in is not None:
                    x_v = x_in.rearrange("g n c -> n g c")
                    sp.dma_start(x_sb[:, 0:QG, :], x_v[:, 0:QG, :]).then_inc(s_x, 16)
                for j, w in enumerate((Wq, Wk, Wv, Wo)):
                    sp.dma_start(w_raw[:, j, :], w).then_inc(s_w, 16)
                if normed:
                    for j, v in enumerate((bq, bk, bv)):
                        sp.dma_start(cols_in[:, j:j + 1], col(v)).then_inc(s_w, 16)
                    sp.dma_start(gamma[:], row(g_in)).then_inc(s_w, 16)
                    sp.dma_start(beta[:], row(b_in)).then_inc(s_w, 16)
                sp.dma_start(out_bias[:], row(bo)).then_inc(s_w, 16)
                for k in range(2):
                    sp.dma_start(adj_in[:, k], adj_v[:, k * QG:(k + 1) * QG, :]).then_inc(s_adj[k], 16)
                if x_in is not None:
                    sp.wait_ge(s_x, 16)
                    sp.dma_start(x_sb[:, QG:N_GRAPHS, :], x_v[:, QG:N_GRAPHS, :]).then_inc(s_x, 16)
                with sp.Fori(1, QUADS // 2) as j:
                    for par in range(2):
                        k = 2 * j + par
                        sp.wait_ge(s_mask, k - 1)
                        sp.dma_start(adj_in[:, par], adj_v[:, bass.ds(k * QG, QG), :]).then_inc(s_adj[par], 16)

            @block.gpsimd
            def _(pool):
                nc.gpsimd.memset(head_mask[:], 1.0).then_inc(s_hm, 1)
                nc.gpsimd.memset(v_ones[:], 1.0).then_inc(s_hm, 1)
                pool.wait_ge(s_hm, 2)
                nc.gpsimd.affine_select(out=head_mask[:], in_=head_mask[:], compare_op=ALU.is_ge, fill=0.0,
                                        base=0, pattern=[[-D, heads]], channel_multiplier=1).then_inc(s_hm, 1)
                pool.wait_ge(s_hm, 3)
                nc.gpsimd.affine_select(out=head_mask[:], in_=head_mask[:], compare_op=ALU.is_ge, fill=0.0,
                                        base=D - 1, pattern=[[D, heads]], channel_multiplier=-1).then_inc(s_hm, 1)
                pool.wait_ge(s_prep, n_prep)

                def body(j, par):
                    k = 2 * j + par
                    if live(k + 2, QUADS):
                        pool.wait_ge(s_var, k + 3)
                        nc.gpsimd.tensor_tensor(rstd[:], var[:], minus_half[:, 0:QG], ALU.pow).then_inc(s_rstd, 1)
                    if normed and live(k - 2, QUADS):
                        x_quad = x_sb[:, bass.ds((k - 2) * QG, QG), :]
                        pool.wait_ge(s_fn, k - 1)
                        nc.gpsimd.tensor_tensor(proj_n[:], proj_n[:], quad_row(gamma), ALU.mult).then_inc(s_fp, 1)
                        pool.wait_ge(s_fp, 2 * (k - 2) + 1)
                        nc.gpsimd.tensor_tensor(proj_n[:], proj_n[:], quad_row(beta), ALU.add).then_inc(s_fp, 1)
                        pool.wait_ge(s_fp, 2 * (k - 2) + 2)
                        nc.gpsimd.tensor_tensor(x_quad, x_quad, proj_n[:], ALU.add).then_inc(s_done, 1)
                    if live(k + 2, QUADS):
                        pool.wait_ge(s_adj[par], 16 * (j + 2))
                        wait(pool, s_s, (k + 1) * NU)
                    if normed and live(k - 1, QUADS):
                        pool.wait_ge(s_fvar, k)
                        nc.gpsimd.tensor_tensor(rstd_o[:], var_o[:], minus_half[:, 0:QG], ALU.pow).then_inc(s_frstd, 1)
                    if not normed and live(k - 1, QUADS):
                        x_quad = x_sb[:, bass.ds((k - 1) * QG, QG), :]
                        pool.wait_ge(s_fin, k)
                        nc.gpsimd.tensor_tensor(x_quad, x_quad, quad_row(out_bias), ALU.add).then_inc(s_done, 1)
                    if live(k + 2, QUADS):
                        nc.gpsimd.tensor_scalar(mask[:, par], adj_in[:, par], 0.0, MASKED, masked_op,
                                                ALU.mult).then_inc(s_mask, 1)

                quads(pool, body)
                pool.wait_ge(s_done, QUADS)

            @block.vector
            def _(dve):
                chain = [0]

                def link(ins):
                    chain[0] += 1
                    ins.then_inc(s_prep, 1)
                    dve.wait_ge(s_prep, chain[0])

                dve.wait_ge(s_w, n_weights)
                for i, w in enumerate((w_q, w_k, w_v, w_o)):
                    if transposed:
                        dve.wait_ge(s_wt, 1)
                    link(nc.vector.tensor_copy(w[:], p_a[:, i * P:(i + 1) * P] if transposed else w_raw[:, i, :]))
                if normed:
                    link(nc.vector.tensor_copy(bv_bc[:], cols_in[:, 2:3].broadcast_to([P, P])))
                    dve.wait_ge(s_wt, 2)
                    link(nc.vector.tensor_tensor(out_bias[:], out_bias[:], p_b[:, 0:P], ALU.add))
                assert chain[0] == n_prep
                dve.wait_ge(s_hm, 4)

                def stats_x(k):
                    if x_in is not None:
                        dve.wait_ge(s_x, 16 if isinstance(k, int) and k == 0 else 32)
                    wait(dve, s_xn, k)
                    for g in range(0, QG, 2):
                        last = nc.vector.bn_stats(stats[:, g // 2].rearrange("p a s -> p (a s)"),
                                                  x_sb[:, bass.ds(k * QG + g, 2), :].rearrange("p a c -> p c a"))
                    last.then_inc(s_ln, 1)
                    dve.wait_ge(s_ln, k + 1)
                    nc.vector.tensor_scalar(var[:].rearrange("p (g a) -> p g a", a=2), stats[:, :, :, 2],
                                            1.0 / P, EPS, ALU.mult, ALU.add).then_inc(s_var, 1)

                def normalise_x(k):
                    dve.wait_ge(s_rstd, k + 1)
                    wait(dve, s_xt, k)
                    for g in range(QG):
                        last = nc.vector.tensor_scalar(xn[:, g, :], x_sb[:, k * QG + g, :], stats[:, g // 2, g % 2, 1:2],
                                                       rstd[:, g:g + 1], ALU.subtract, ALU.mult)
                    last.then_inc(s_xn, 1)

                def keys(k, par, some):
                    if some[0] == 0:
                        dve.wait_ge(s_kmm, k + 1)
                        wait(dve, s_s, (k - 1) * NU)
                    product = p_a[:].rearrange("p (g m) -> p g m", g=QG)
                    for h in some:
                        if normed:
                            last = nc.vector.tensor_scalar(k_heads[:, par, :, h, :], product, cols_in[:, 1:2],
                                                           head_mask[:, h:h + 1], ALU.add, ALU.mult)
                        else:
                            last = nc.vector.tensor_scalar(k_heads[:, par, :, h, :], product,
                                                           head_mask[:, h:h + 1], None, ALU.mult)
                    if some[-1] == heads - 1:
                        last.then_inc(s_k, 1)

                def maximum(n, b):
                    dve.wait_ge(s_s, n + 1)
                    nc.vector.tensor_reduce(out=row_max[:, b], in_=p_s[:, b], axis=AX.X, op=ALU.max).then_inc(s_max, 1)
                    dve.wait_ge(s_max, n + 1)
                    wait(dve, s_exp, n - 1)
                    nc.vector.tensor_scalar(neg_max[:, b], row_max[:, b], -SCALE, None, ALU.mult).then_inc(s_neg, 1)

                def normalise(k, u):
                    n, graph = k * NU + u, k * QG + u // UG
                    h0 = (u % UG) * HU
                    dve.wait_ge(s_pv, n + 1)
                    nc.vector.reciprocal(rden[:], p_pv[:, :, D]).then_inc(s_rden, 1)
                    dve.wait_ge(s_rden, n + 1)
                    if u % UG == 0:
                        wait(dve, s_ct, graph - 1)
                    dst = context[:, u // UG % 2, h0 * D:(h0 + HU) * D]
                    nc.vector.tensor_tensor(dst.rearrange("p (h c) -> p h c", h=HU), p_pv[:, :, 0:D],
                                            rden[:].rearrange("p (h a) -> p h a", a=1).broadcast_to([P, HU, D]),
                                            ALU.mult).then_inc(s_norm, 1)

                def take_projection(k):
                    dve.wait_ge(s_o, (k + 1) * QG)
                    if not normed:
                        x_quad = x_sb[:, bass.ds(k * QG, QG), :]
                        nc.vector.tensor_tensor(x_quad, x_quad, p_o[:], ALU.add).then_inc(s_fin, 1)
                        return
                    wait(dve, s_fn, k)
                    nc.vector.tensor_tensor(proj[:], p_o[:], quad_row(out_bias), ALU.add).then_inc(s_fin, 1)
                    dve.wait_ge(s_fin, k + 1)
                    for g in range(0, QG, 2):
                        last = nc.vector.bn_stats(stats_o[:, g // 2].rearrange("p a s -> p (a s)"),
                                                  proj[:, g:g + 2, :].rearrange("p a c -> p c a"))
                    last.then_inc(s_fln, 1)
                    dve.wait_ge(s_fln, k + 1)
                    nc.vector.tensor_scalar(var_o[:].rearrange("p (g a) -> p g a", a=2), stats_o[:, :, :, 2],
                                            1.0 / P, EPS, ALU.mult, ALU.add).then_inc(s_fvar, 1)

                def normalise_projection(k):
                    dve.wait_ge(s_frstd, k + 1)
                    wait(dve, s_done, k)
                    for g in range(QG):
                        last = nc.vector.tensor_scalar(proj_n[:, g, :], proj[:, g, :], stats_o[:, g // 2, g % 2, 1:2],
                                                       rstd_o[:, g:g + 1], ALU.subtract, ALU.mult)
                    last.then_inc(s_fn, 1)

                def body(j, par):
                    k = 2 * j + par
                    for u in range(NU):
                        n = k * NU + u
                        if u == 3 and live(k - 1, QUADS):
                            take_projection(k - 1)
                        if live(n + 2, TOTAL):
                            maximum(n + 2, u % 2)
                        if live(n - 1, TOTAL):
                            normalise(*unit(k, u, -1))
                        some = [h for h in range(heads) if h * KEY_SLOTS // heads == u]
                        if some and live(k + 1, QUADS):
                            keys(k + 1, 1 - par, some)
                        if u == 0 and live(k + 2, QUADS):
                            stats_x(k + 2)
                        if u == 1 and normed and live(k - 2, QUADS):
                            normalise_projection(k - 2)
                        if u == NU // 2 and live(k + 2, QUADS):
                            normalise_x(k + 2)

                quads(dve, body)

            @block.tensor
            def _(pe):
                pe.wait_ge(s_w, n_weights)
                if transposed:
                    for i in range(4):
                        last = nc.tensor.transpose(p_a[:, i * P:(i + 1) * P], w_raw[:, i, :], ident[:])
                    last.then_inc(s_wt, 1)
                    pe.wait_ge(s_prep, 5)
                    nc.tensor.matmul(p_b[:, 0:P], bv_bc[:], w_o[:], start=True, stop=True).then_inc(s_wt, 1)
                pe.wait_ge(s_prep, n_prep)

                def scores(k, par, u):
                    n, g, h0 = k * NU + u, u // UG, (u % UG) * HU
                    if u == 0:
                        pe.wait_ge(s_mask, k + 1)
                        pe.wait_ge(s_q, k + 1)
                        pe.wait_ge(s_k, k + 1)
                    wait(pe, s_exp, n - 1)
                    edges = mask[:, par, g:g + 1, :].broadcast_to([P, HU, P])
                    nc.tensor.matmul(p_s[:, u % 2], ident_bf[:], edges, start=True, stop=False)
                    nc.tensor.matmul(p_s[:, u % 2], q_t[:, par, g * P:(g + 1) * P],
                                     k_heads[:, par, g, h0:h0 + HU, :], start=False, stop=True).then_inc(s_s, 1)

                def transpose_prob(n, b):
                    pe.wait_ge(s_exp, n + 1)
                    wait(pe, s_ptc, n)
                    for h in range(HU):
                        last = nc.tensor.transpose(p_pt[:, h, :], prob[:, b, h, :], ident[:])
                    last.then_inc(s_tr, 1)

                def context_product(k, par, u):
                    n, g, h0 = k * NU + u, u // UG, (u % UG) * HU
                    if u == 0:
                        pe.wait_ge(s_v, k + 1)
                    pe.wait_ge(s_ptc, n + 1)
                    wait(pe, s_norm, n)
                    for h in range(HU):
                        last = nc.tensor.matmul(p_pv[:, h, :], prob_t[:, u % 2, h, :], v_ones[:, par, g, h0 + h, :],
                                                start=True, stop=True)
                    last.then_inc(s_pv, 1)

                def transpose_context(k, u):
                    graph = k * QG + u // UG
                    pe.wait_ge(s_norm, k * NU + u + 1)
                    wait(pe, s_ctc, graph)
                    nc.tensor.transpose(p_ct[:], context[:, u // UG % 2, :], ident[:]).then_inc(s_ct, 1)

                def project(k, u):
                    g = u // UG
                    pe.wait_ge(s_ctc, k * QG + g + 1)
                    if g == 0:
                        wait(pe, s_fin, k)
                    nc.tensor.matmul(p_o[:, g, :], context_t[:, g % 2, :], w_o[:], start=True, stop=True).then_inc(s_o, 1)

                def body(j, par):
                    k = 2 * j + par
                    for u in range(NU):
                        n = k * NU + u
                        if live(n + 2, TOTAL):
                            k2, u2 = unit(k, u, 2)
                            scores(k2, par if u2 >= 2 else 1 - par, u2)
                        if live(n, TOTAL):
                            transpose_prob(n, u % 2)
                        if live(n - 1, TOTAL):
                            k1, u1 = unit(k, u, -1)
                            context_product(k1, par if u else 1 - par, u1)
                        if live(n - 2, TOTAL) and (u - 2) % UG == UG - 1:
                            transpose_context(*unit(k, u, -2))
                        if live(n - 3, TOTAL) and (u - 3) % UG == UG - 1:
                            project(*unit(k, u, -3))
                        if u == 0 and live(k + 1, QUADS):
                            pe.wait_ge(s_xtc, k + 2)
                            wait(pe, s_v, k + 1)
                            nc.tensor.matmul(p_a[:], w_k[:], xn_t[:, 1 - par], start=True, stop=True).then_inc(s_kmm, 1)
                            nc.tensor.matmul(p_b[:], w_q[:], xn_t[:, 1 - par], start=True, stop=True).then_inc(s_qmm, 1)
                        if u == 1 and live(k + 1, QUADS):
                            pe.wait_ge(s_q, k + 2)
                            for g in range(QG):
                                last = nc.tensor.matmul(p_b[:, g * P:(g + 1) * P], xn_t[:, 1 - par, g * P:(g + 1) * P],
                                                        w_v[:], start=True, stop=True)
                            last.then_inc(s_vmm, 1)
                        if u == NU - 1 and live(k + 2, QUADS):
                            pe.wait_ge(s_xn, k + 3)
                            wait(pe, s_k, k + 2)
                            for g in range(QG):
                                last = nc.tensor.transpose(p_a[:, g * P:(g + 1) * P], xn[:, g, :], ident[:])
                            last.then_inc(s_xt, 1)

                quads(pe, body)

            @block.scalar
            def _(act):
                act.wait_ge(s_hm, 2)
                act.wait_ge(s_prep, n_prep)

                def exponentials(k, u):
                    n = k * NU + u
                    act.wait_ge(s_neg, n + 1)
                    wait(act, s_tr, n - 1)
                    for h in range(HU):
                        last = nc.scalar.activation(prob[:, u % 2, h, :], p_s[:, u % 2, h, :], ACT.Exp,
                                                    bias=neg_max[:, u % 2, h:h + 1], scale=SCALE)
                    last.then_inc(s_exp, 1)

                def body(j, par):
                    k = 2 * j + par
                    for u in range(NU):
                        n = k * NU + u
                        if live(n + 1, TOTAL):
                            exponentials(*unit(k, u, 1))
                        if live(n, TOTAL):
                            act.wait_ge(s_tr, n + 1)
                            wait(act, s_pv, n - 1)
                            nc.scalar.copy(prob_t[:, u % 2], p_pt[:]).then_inc(s_ptc, 1)
                        if live(n - 2, TOTAL) and (u - 2) % UG == UG - 1:
                            k2, u2 = unit(k, u, -2)
                            g = u2 // UG
                            act.wait_ge(s_ct, k2 * QG + g + 1)
                            wait(act, s_o, k2 * QG + g - 1)
                            nc.scalar.copy(context_t[:, g % 2, :], p_ct[:]).then_inc(s_ctc, 1)
                        if u == 0 and live(k + 1, QUADS):
                            act.wait_ge(s_qmm, k + 2)
                            wait(act, s_s, k * NU)
                            if normed:
                                nc.scalar.activation(q_t[:, 1 - par], p_b[:], ACT.Identity,
                                                     bias=cols_in[:, 0:1]).then_inc(s_q, 1)
                            else:
                                nc.scalar.copy(q_t[:, 1 - par], p_b[:]).then_inc(s_q, 1)
                        if u == 1 and live(k + 1, QUADS):
                            act.wait_ge(s_vmm, k + 2)
                            wait(act, s_pv, k * NU)
                            nc.scalar.copy(v_ones[:, 1 - par, :, :, 0:D],
                                           p_b[:].rearrange("p (g h c) -> p g h c", g=QG, h=heads)).then_inc(s_v, 1)
                        if u == NU - 1 and live(k + 2, QUADS):
                            act.wait_ge(s_xt, k + 3)
                            wait(act, s_vmm, k + 1)
                            nc.scalar.copy(xn_t[:, par], p_a[:]).then_inc(s_xtc, 1)

                quads(act, body)


def mixture_ffn(nc, env, x_sb, router_w, w1, b1, w2, b2, N_TILES=128):
    E = 8
    GT = 4
    GROUP = GT * P
    GROUPS = N_TILES // GT
    TOTAL = GROUPS * E
    GONE = -3.0e38

    with ExitStack() as ctx:
        sb = lambda n, s, d=F32: ctx.enter_context(nc.sbuf_tensor("m_" + n, s, d))
        pb = lambda n, s, d=F32: ctx.enter_context(nc.psum_tensor("m_" + n, s, d))
        sem = lambda n: ctx.enter_context(nc.semaphore("m_" + n))
        ident, minus_half = env["ident"], env["minus_half"]

        w1_sb = sb("w1_sb", [P, E, P])
        w2_sb = sb("w2_sb", [P, E, P])
        rows_in = sb("rows_in", [2 * E, P])
        cols = sb("cols", [P, 2, E])
        b2_blocks = sb("b2_blocks", [GT * E, GT, P])
        euler = sb("euler", [P, GT])
        index = sb("index", [P, GT, E])
        stats = sb("stats", [P, GT // 2, 2, 3])
        var = sb("var", [P, GT])
        rstd = sb("rstd", [P, GT])
        xn = sb("xn", [P, GT, P])
        xn_t = sb("xn_t", [P, 2, GROUP])
        hidden = sb("hidden", [P, 2, GROUP])
        logits = sb("logits", [P, GT, E])
        others = sb("others", [P, GT, E])
        same = sb("same", [P, GT, E])
        place = sb("place", [P, GT, E])
        first = sb("first", [P, GT, E])
        second = sb("second", [P, GT, E])
        top = sb("top", [P, 2, GT])
        where = sb("where", [P, 2, GT])
        gap = sb("gap", [P, GT])
        ratio = sb("ratio", [P, GT])
        total = sb("total", [P, GT])
        ones = sb("ones", [P, GT])
        minus_one = sb("minus_one", [P, GT])
        weighted = sb("weighted", [P, 2, GT, E])
        share = sb("share", [P, 2, GT])
        combine = sb("combine", [P, 2, GT, E])
        combine_t = sb("combine_t", [GT * E, P])

        p_h = pb("p_h", [P, 2, GROUP])
        p_y = pb("p_y", [P, 2, GT, P])
        p_xt = pb("p_xt", [P, GROUP])
        p_lg = pb("p_lg", [P, GT, E])
        p_ct = pb("p_ct", [GT * E, P])
        p_b2 = pb("p_b2", [P, GT, P])

        s_w = sem("weights_loaded")
        s_b2z = sem("b2_zeroed")
        s_const = sem("constants_ready")
        s_rt = sem("rows_transposed")
        s_cols = sem("cols_ready")
        s_ln = sem("ln_chain")
        s_var = sem("var_ready")
        s_rstd = sem("rstd_ready")
        s_xn = sem("xn_ready")
        s_xadd = sem("xn_added")
        s_xt = sem("xn_transposed")
        s_xtc = sem("xn_t_ready")
        s_lg = sem("logits_product")
        s_lgc = sem("logits_ready")
        s_route = sem("routing_chain")
        s_gap = sem("gap_ready")
        s_share = sem("share_chain")
        s_comb = sem("combine_ready")
        s_ct = sem("combine_transposed")
        s_ctc = sem("combine_t_ready")
        s_b2 = sem("b2_product")
        s_b2a = sem("b2_added")
        s_h = sem("hidden_product")
        s_gelu = sem("hidden_ready")
        s_y = sem("output_product")
        s_acc = sem("output_added")

        def live(q, limit):
            return not isinstance(q, int) or 0 <= q < limit

        def wait(eng, s, value):
            if not isinstance(value, int) or value > 0:
                eng.wait_ge(s, value)

        def groups(eng, body):
            body(-2, 0)
            body(-1, 1)
            body(0, 0)
            body(1, 1)
            with eng.Fori(1, GROUPS // 2 - 1) as j:
                body(2 * j, 0)
                body(2 * j + 1, 1)
            body(GROUPS - 2, 0)
            body(GROUPS - 1, 1)

        per_tile = lambda t: t.rearrange("p (g a) -> p g a", a=1).broadcast_to([P, GT, E])
        ROUTE = 11

        with nc.Block() as block:
            @block.sync
            def _(sp):
                sp.dma_start(rows_in[0:E, :], router_w).then_inc(s_w, 16)
                sp.dma_start(rows_in[E:2 * E, :], b1).then_inc(s_w, 16)
                sp.dma_start(w1_sb[:], w1.rearrange("e c f -> c e f")).then_inc(s_w, 16)
                sp.dma_start(w2_sb[:], w2.rearrange("e f d -> f e d")).then_inc(s_w, 16)
                sp.wait_ge(s_b2z, 1)
                for t in range(GT):
                    sp.dma_start(b2_blocks[t * E:(t + 1) * E, t, :], b2).then_inc(s_w, 16)
                sp.wait_ge(s_w, 16 * 8)

            @block.gpsimd
            def _(pool):
                nc.gpsimd.memset(b2_blocks[:], 0.0).then_inc(s_b2z, 1)
                nc.gpsimd.memset(euler[:], float(np.e)).then_inc(s_const, 1)
                nc.gpsimd.memset(ones[:], 1.0).then_inc(s_const, 1)
                nc.gpsimd.memset(minus_one[:], -1.0).then_inc(s_const, 1)
                for e in range(E):
                    nc.gpsimd.memset(index[:, :, e], float(e - E)).then_inc(s_const, 1)
                pool.wait_ge(s_const, E + 3)

                def body(k, par):
                    if live(k + 1, GROUPS):
                        g = k + 1
                        pool.wait_ge(s_gap, g + 1)
                        nc.gpsimd.tensor_tensor(ratio[:], euler[:], gap[:], ALU.pow).then_inc(s_share, 1)
                        pool.wait_ge(s_share, 6 * g + 1)
                        nc.gpsimd.tensor_tensor(total[:], ratio[:], ones[:], ALU.add).then_inc(s_share, 1)
                        pool.wait_ge(s_share, 6 * g + 2)
                        nc.gpsimd.tensor_tensor(share[:, 0], total[:], minus_one[:], ALU.pow).then_inc(s_share, 1)
                        pool.wait_ge(s_share, 6 * g + 3)
                        nc.gpsimd.tensor_tensor(share[:, 1], ratio[:], share[:, 0], ALU.mult).then_inc(s_share, 1)
                        pool.wait_ge(s_share, 6 * g + 4)
                        pool.wait_ge(s_route, (g + 1) * ROUTE)
                        nc.gpsimd.tensor_tensor(weighted[:, 0], first[:], per_tile(share[:, 0]), ALU.mult).then_inc(s_share, 1)
                        nc.gpsimd.tensor_tensor(weighted[:, 1], second[:], per_tile(share[:, 1]), ALU.mult).then_inc(s_share, 1)
                        pool.wait_ge(s_share, 6 * g + 6)
                        wait(pool, s_acc, (g - 1) * E)
                        wait(pool, s_ct, g - 1)
                        nc.gpsimd.tensor_tensor(combine[:, 1 - par], weighted[:, 0], weighted[:, 1], ALU.add).then_inc(s_comb, 1)

                    if live(k + 2, GROUPS):
                        g = k + 2
                        pool.wait_ge(s_var, g + 1)
                        nc.gpsimd.tensor_tensor(rstd[:], var[:], minus_half[:, 0:GT], ALU.pow).then_inc(s_rstd, 1)
                        x_group = x_sb[:, bass.ds(g * GT, GT), :]
                        pool.wait_ge(s_xn, g + 1)
                        nc.gpsimd.tensor_tensor(x_group, x_group, xn[:], ALU.add).then_inc(s_xadd, 1)

                groups(pool, body)

            @block.vector
            def _(dve):
                dve.wait_ge(s_rt, 1)
                nc.vector.tensor_copy(cols[:].rearrange("p a e -> p (a e)"), p_lg[:].rearrange("p g e -> p (g e)")[:, 0:2 * E]).then_inc(s_cols, 1)

                dve.wait_ge(s_const, E + 3)

                def route(g, i):
                    done = g * ROUTE + i
                    if i == 0:
                        dve.wait_ge(s_lgc, g + 1)
                        wait(dve, s_comb, g)
                    elif i < ROUTE:
                        dve.wait_ge(s_route, done)
                    if i == 0:
                        op = nc.vector.tensor_reduce(out=top[:, 0], in_=logits[:], axis=AX.X, op=ALU.max)
                    elif i == 1:
                        op = nc.vector.tensor_tensor(same[:], logits[:], per_tile(top[:, 0]), ALU.is_equal)
                    elif i == 2:
                        op = nc.vector.tensor_tensor(place[:], same[:], index[:], ALU.mult)
                    elif i == 3:
                        op = nc.vector.tensor_reduce(out=where[:, 0], in_=place[:], axis=AX.X, op=ALU.min)
                    elif i == 4:
                        op = nc.vector.tensor_tensor(first[:], index[:], per_tile(where[:, 0]), ALU.is_equal)
                    elif i == 5:
                        op = nc.vector.scalar_tensor_tensor(out=others[:], in0=first[:], scalar=GONE, in1=logits[:],
                                                            op0=ALU.mult, op1=ALU.add)
                    elif i == 6:
                        op = nc.vector.tensor_reduce(out=top[:, 1], in_=others[:], axis=AX.X, op=ALU.max)
                    elif i == 7:
                        nc.vector.tensor_tensor(gap[:], top[:, 1], top[:, 0], ALU.subtract).then_inc(s_gap, 1)
                        op = nc.vector.tensor_tensor(same[:], others[:], per_tile(top[:, 1]), ALU.is_equal)
                    elif i == 8:
                        op = nc.vector.tensor_tensor(place[:], same[:], index[:], ALU.mult)
                    elif i == 9:
                        op = nc.vector.tensor_reduce(out=where[:, 1], in_=place[:], axis=AX.X, op=ALU.min)
                    elif i == 10:
                        op = nc.vector.tensor_tensor(second[:], index[:], per_tile(where[:, 1]), ALU.is_equal)
                    else:
                        return
                    op.then_inc(s_route, 1)

                def body(k, par):
                    for e in range(E):
                        n = k * E + e
                        if e == 5 and live(k + 2, GROUPS):
                            g = k + 2
                            wait(dve, s_xn, g)
                            for t in range(0, GT, 2):
                                last = nc.vector.bn_stats(stats[:, t // 2].rearrange("p a s -> p (a s)"),
                                                          x_sb[:, bass.ds(g * GT + t, 2), :].rearrange("p a c -> p c a"))
                            last.then_inc(s_ln, 1)
                            dve.wait_ge(s_ln, g + 1)
                            nc.vector.tensor_scalar(var[:].rearrange("p (t a) -> p t a", a=2), stats[:, :, :, 2],
                                                    1.0 / P, EPS, ALU.mult, ALU.add).then_inc(s_var, 1)
                        if e == 7 and live(k + 2, GROUPS):
                            g = k + 2
                            dve.wait_ge(s_rstd, g + 1)
                            wait(dve, s_xt, g)
                            wait(dve, s_xadd, g)
                            for t in range(GT):
                                last = nc.vector.tensor_scalar(xn[:, t, :], x_sb[:, g * GT + t, :], stats[:, t // 2, t % 2, 1:2],
                                                               rstd[:, t:t + 1], ALU.subtract, ALU.mult)
                            last.then_inc(s_xn, 1)
                        if live(k, GROUPS):
                            if e == 0:
                                dve.wait_ge(s_comb, k + 1)
                                dve.wait_ge(s_xadd, k + 1)
                            dve.wait_ge(s_y, n + 1)
                            if e == 4:
                                dve.wait_ge(s_b2a, k + 1)
                            wait(dve, s_acc, n)
                        for t in range(GT):
                            if live(k, GROUPS):
                                x_tile = x_sb[:, k * GT + t, :]
                                last = nc.vector.scalar_tensor_tensor(out=x_tile, in0=p_y[:, e % 2, t, :],
                                                                      scalar=combine[:, par, t, e:e + 1], in1=x_tile,
                                                                      op0=ALU.mult, op1=ALU.add)
                                if t == GT - 1:
                                    last.then_inc(s_acc, 1)
                            if 2 <= e < 5 and live(k + 1, GROUPS):
                                route(k + 1, (e - 2) * GT + t)
                        if e == 3 and live(k, GROUPS):
                            dve.wait_ge(s_b2, k + 1)
                            dve.wait_ge(s_acc, n + 1)
                            x_group = x_sb[:, bass.ds(k * GT, GT), :]
                            nc.vector.tensor_tensor(x_group, x_group, p_b2[:], ALU.add).then_inc(s_b2a, 1)

                groups(dve, body)

            @block.tensor
            def _(pe):
                pe.wait_ge(s_w, 16 * 8)
                nc.tensor.transpose(p_lg[:].rearrange("p g e -> p (g e)")[:, 0:2 * E], rows_in[:], ident[0:2 * E, 0:2 * E]).then_inc(s_rt, 1)
                pe.wait_ge(s_cols, 1)

                def hidden_product(k, par, e):
                    n = k * E + e
                    if e == 0:
                        pe.wait_ge(s_xtc, k + 1)
                    wait(pe, s_gelu, n - 1)
                    nc.tensor.matmul(p_h[:, e % 2, :], w1_sb[:, e, :], xn_t[:, par, :],
                                     start=True, stop=True).then_inc(s_h, 1)

                def output_product(k, e):
                    n = k * E + e
                    pe.wait_ge(s_gelu, n + 1)
                    wait(pe, s_acc, n - 1)
                    for t in range(GT):
                        last = nc.tensor.matmul(p_y[:, e % 2, t, :], hidden[:, e % 2, t * P:(t + 1) * P],
                                                w2_sb[:, e, :], start=True, stop=True)
                    last.then_inc(s_y, 1)

                def body(k, par):
                    g = k + 1
                    for e in range(E):
                        if e < E - 1:
                            if live(k, GROUPS):
                                hidden_product(k, par, e + 1)
                        elif live(g, GROUPS):
                            hidden_product(g, 1 - par, 0)
                        if live(k, GROUPS):
                            output_product(k, e)
                        if e == 0 and live(g, GROUPS):
                            pe.wait_ge(s_xn, g + 1)
                            wait(pe, s_xtc, g)
                            for t in range(GT):
                                last = nc.tensor.transpose(p_xt[:, t * P:(t + 1) * P], xn[:, t, :], ident[:])
                            last.then_inc(s_xt, 1)
                        if e == 1 and live(g, GROUPS):
                            pe.wait_ge(s_xtc, g + 1)
                            wait(pe, s_lgc, g)
                            for t in range(GT):
                                last = nc.tensor.matmul(p_lg[:, t, :], xn_t[:, 1 - par, t * P:(t + 1) * P], cols[:, 0, :],
                                                        start=True, stop=True)
                            last.then_inc(s_lg, 1)
                        if e == 1 and live(k, GROUPS):
                            pe.wait_ge(s_comb, k + 1)
                            wait(pe, s_ctc, k)
                            nc.tensor.transpose(p_ct[:], combine[:, par].rearrange("p g e -> p (g e)"),
                                                ident[:]).then_inc(s_ct, 1)
                        if e == 2 and live(k, GROUPS):
                            pe.wait_ge(s_ctc, k + 1)
                            wait(pe, s_b2a, k)
                            nc.tensor.matmul(p_b2[:], combine_t[:], b2_blocks[:], start=True, stop=True).then_inc(s_b2, 1)

                groups(pe, body)

            @block.scalar
            def _(act):
                act.wait_ge(s_cols, 1)

                def gelu(k, e):
                    n = k * E + e
                    act.wait_ge(s_h, n + 1)
                    wait(act, s_y, n - 1)
                    nc.scalar.activation(hidden[:, e % 2, :], p_h[:, e % 2, :], ACT.Gelu,
                                         bias=cols[:, 1, e:e + 1]).then_inc(s_gelu, 1)

                def body(k, par):
                    g = k + 1
                    for e in range(E):
                        if e < E - 1:
                            if live(k, GROUPS):
                                gelu(k, e + 1)
                        elif live(g, GROUPS):
                            gelu(g, 0)
                        if e == 0 and live(g, GROUPS):
                            act.wait_ge(s_xt, g + 1)
                            wait(act, s_h, (g - 1) * E)
                            wait(act, s_lg, g - 1)
                            nc.scalar.copy(xn_t[:, 1 - par, :], p_xt[:]).then_inc(s_xtc, 1)
                        if e == 1 and live(g, GROUPS):
                            act.wait_ge(s_lg, g + 1)
                            wait(act, s_comb, g)
                            nc.scalar.copy(logits[:], p_lg[:]).then_inc(s_lgc, 1)
                        if e == 1 and live(k, GROUPS):
                            act.wait_ge(s_ct, k + 1)
                            wait(act, s_b2, k)
                            nc.scalar.copy(combine_t[:], p_ct[:]).then_inc(s_ctc, 1)

                groups(act, body)


def recurrent_ffn(nc, env, x_sb, out_dram, ln_w, ln_b, w_dram, b_dram, N_TILES=128, ITERS=30):
    FLIGHT = 4
    CT = 8
    UT = 4
    UNITS = CT // UT
    CHUNK, UNIT = CT * P, UT * P
    PT = FLIGHT * CT
    PASSES = N_TILES // PT
    STEPS = ITERS * FLIGHT
    LAST = STEPS - FLIGHT

    with ExitStack() as ctx:
        sb = lambda n, s, d=F32: ctx.enter_context(nc.sbuf_tensor("d_" + n, s, d))
        pb = lambda n, s, d=F32: ctx.enter_context(nc.psum_tensor("d_" + n, s, d))
        sem = lambda n: ctx.enter_context(nc.semaphore("d_" + n))
        ident, ident_bf, minus_half = env["ident"], env["ident_bf"], env["minus_half"]

        w_rows = sb("w_rows", [P, P])
        w_centred = sb("w_centred", [P, P])
        w_main = sb("w_main", [P, P])
        lnw_bc = sb("lnw_bc", [P, P])
        lnb_bc = sb("lnb_bc", [P, P])
        row_sum = sb("row_sum", [P, 1])
        bias = sb("bias", [P, 1])
        b_col = sb("b_col", [P, 1])
        pick = sb("pick", [P, CT, P], BF16)
        xn = sb("xn", [P, PT, P])
        th = sb("th", [P, 2, CHUNK])
        g = sb("g", [P, FLIGHT, CHUNK])
        gs = sb("gs", [P, 2, CHUNK])
        stats = sb("stats", [P, 2, CT // 2, 2, 3])
        var = sb("var", [P, 2, CT])
        rstd = sb("rstd", [P, CT])
        zeros = sb("zeros", [P, CT])
        rem = sb("rem", [P, CT])
        parts = sb("parts", [P, 2, P // CT, CT], BF16)
        parts_t = sb("parts_t", [P, 2, P], BF16)
        stats_x = sb("stats_x", [P, PT // 2, 2, 3])
        var_x = sb("var_x", [P, PT])
        rstd_x = sb("rstd_x", [P, PT])
        res = sb("res", [P, UNITS, UNIT])
        out_sb = sb("out_sb", [P, UNITS, UNIT])

        p_gt = pb("p_gt", [P, CHUNK])
        p_rb = pb("p_rb", [P, CHUNK])
        p_y = pb("p_y", [P, CHUNK])
        p_back = pb("p_back", [P, UNIT])
        p_rt = pb("p_rt", [P, 2, P], BF16)

        s_load = sem("weights_loaded")
        s_prep = sem("prep_chain")
        s_prep_pe = sem("prep_transposed")
        s_pick = sem("pick_chain")
        s_zero = sem("parts_zeroed")
        s_pool = sem("pool_chain")
        s_xchain = sem("x_chain")
        s_xvar = sem("x_var_ready")
        s_xrstd = sem("x_rstd_ready")
        s_xn = sem("xn_ready")
        s_gt = sem("g_transposed")
        s_bn = sem("stats_ready")
        s_var = sem("variance_ready")
        s_parts = sem("parts_ready")
        s_rt = sem("parts_transposed")
        s_rts = sem("parts_evacuated")
        s_rb = sem("rstd_broadcast")
        s_gs = sem("g_scaled")
        s_y = sem("product_ready")
        s_tanh = sem("tanh_ready")
        s_u = sem("u_ready")
        s_g = sem("g_ready")
        s_res = sem("result_evacuated")
        s_back = sem("result_transposed")
        s_sum = sem("result_summed")
        s_out = [sem(f"result_stored_{u}") for u in range(UNITS)]

        def steps(p, i):
            return p * STEPS + i + 1

        def units(p, i, u=UNITS - 1):
            return (p * STEPS + i) * UNITS + u + 1

        def products(p, i, u=UNITS - 1):
            return (p * (STEPS + FLIGHT) + i + FLIGHT) * UNITS + u + 1

        def results(p, i, u=UNITS - 1):
            return (p * FLIGHT + i - LAST) * UNITS + u + 1

        def wait(eng, s, value):
            if not isinstance(value, int) or value > 0:
                eng.wait_ge(s, value)

        def passes(eng, body):
            body(0)
            with eng.Fori(1, PASSES) as p:
                body(p)

        POOL_OPS = 4
        cols = lambda u: slice(u * UNIT, (u + 1) * UNIT)
        out_v = out_dram.rearrange("g n c -> n g c")

        with nc.Block() as block:
            @block.sync
            def _(sp):
                sp.dma_start(w_rows[:], w_dram).then_inc(s_load, 16)
                sp.dma_start(lnw_bc[:], ln_w.rearrange("(a c) -> a c", a=1).broadcast_to([P, P])).then_inc(s_load, 16)
                sp.dma_start(lnb_bc[:], ln_b.rearrange("(a c) -> a c", a=1).broadcast_to([P, P])).then_inc(s_load, 16)
                sp.dma_start(b_col[:], b_dram.rearrange("(c a) -> c a", a=1)).then_inc(s_load, 16)
                def body(p):
                    for i in range(LAST, STEPS):
                        for u in range(UNITS):
                            sp.wait_ge(s_sum, results(p, i, u))
                            tile = p * PT + (i - LAST) * CT + u * UT
                            sp.dma_start(out_v[:, bass.ds(tile, UT), :],
                                         out_sb[:, u].rearrange("p (t c) -> p t c", t=UT)).then_inc(s_out[u], 16)

                passes(sp, body)
                for u in range(UNITS):
                    sp.wait_ge(s_out[u], 16 * PASSES * FLIGHT)

            @block.gpsimd
            def _(pool):
                nc.gpsimd.memset(pick[:], 0.0).then_inc(s_pick, 1)
                nc.gpsimd.memset(parts[:], 0.0).then_inc(s_zero, 1)
                nc.gpsimd.memset(zeros[:], 0.0).then_inc(s_zero, 1)
                pool.wait_ge(s_zero, 2)
                for part in range(3):
                    pool.wait_ge(s_pick, part + 1)
                    nc.gpsimd.affine_select(out=pick[:], in_=pick[:], compare_op=ALU.not_equal, fill=1.0,
                                            base=-part * CT, pattern=[[-1, CT], [0, P]],
                                            channel_multiplier=1).then_inc(s_pick, 1)

                def step(p, i, k):
                    done = (p * STEPS + i) * POOL_OPS
                    pool.wait_ge(s_var, steps(p, i))
                    nc.gpsimd.tensor_tensor(rstd[:], var[:, k], minus_half[:, 0:CT], ALU.pow).then_inc(s_pool, 1)
                    pool.wait_ge(s_pool, done + 1)
                    wait(pool, s_rt, steps(p, i - 2))
                    nc.gpsimd.tensor_tensor(parts[:, k, 0], rstd[:], zeros[:], ALU.add).then_inc(s_pool, 1)
                    pool.wait_ge(s_pool, done + 2)
                    nc.gpsimd.tensor_tensor(parts[:, k, 1], rstd[:], parts[:, k, 0], ALU.subtract).then_inc(s_pool, 1)
                    nc.gpsimd.tensor_tensor(rem[:], rstd[:], parts[:, k, 0], ALU.subtract).then_inc(s_pool, 1)
                    pool.wait_ge(s_pool, done + 4)
                    nc.gpsimd.tensor_tensor(parts[:, k, 2], rem[:], parts[:, k, 1], ALU.subtract).then_inc(s_parts, 1)

                def body(p):
                    pool.wait_ge(s_xvar, p + 1)
                    nc.gpsimd.tensor_tensor(rstd_x[:], var_x[:], minus_half[:, 0:PT], ALU.pow).then_inc(s_xrstd, 1)
                    step(p, 0, 0)
                    step(p, 1, 1)
                    with pool.Fori(1, STEPS // 2) as pair:
                        step(p, 2 * pair, 0)
                        step(p, 2 * pair + 1, 1)

                passes(pool, body)

            @block.vector
            def _(dve):
                chain = [0]

                def link(ins):
                    chain[0] += 1
                    ins.then_inc(s_prep, 1)
                    dve.wait_ge(s_prep, chain[0])

                dve.wait_ge(s_load, 64)
                link(nc.vector.tensor_tensor(w_centred[:], w_rows[:], lnw_bc[:], ALU.mult))
                link(nc.vector.tensor_reduce(out=row_sum[:], in_=w_centred[:], axis=AX.X, op=ALU.add))
                link(nc.vector.tensor_scalar(row_sum[:], row_sum[:], 1.0 / P, None, ALU.mult))
                link(nc.vector.tensor_scalar(w_centred[:], w_centred[:], row_sum[:], float(np.sqrt(P)),
                                             ALU.subtract, ALU.mult))
                link(nc.vector.tensor_tensor(lnb_bc[:], w_rows[:], lnb_bc[:], ALU.mult))
                link(nc.vector.tensor_reduce(out=bias[:], in_=lnb_bc[:], axis=AX.X, op=ALU.add))
                link(nc.vector.tensor_tensor(bias[:], bias[:], b_col[:], ALU.add))
                dve.wait_ge(s_prep_pe, 1)
                link(nc.vector.tensor_copy(w_main[:], p_back[:, 0:P]))

                def scale_g(p, i, c, u):
                    dve.wait_ge(s_rb, units(p, i, u))
                    dve.wait_ge(s_y, products(p, i - 2, u))
                    nc.vector.tensor_tensor(gs[:, c % 2, cols(u)], g[:, c, cols(u)], p_rb[:, cols(u)],
                                            ALU.mult).then_inc(s_gs, 1)

                def statistics(p, i, k):
                    for u in range(UNITS):
                        dve.wait_ge(s_gt, units(p, i, u))
                        for t in range(u * UT, (u + 1) * UT, 2):
                            last = nc.vector.bn_stats(stats[:, k, t // 2].rearrange("p a s -> p (a s)"),
                                                      p_gt[:, t * P:(t + 2) * P].rearrange("p (a c) -> p c a", a=2))
                        last.then_inc(s_bn, 1)

                def variance(p, i, k):
                    dve.wait_ge(s_bn, units(p, i))
                    wait(dve, s_parts, steps(p, i - 2))
                    nc.vector.tensor_scalar(var[:, k].rearrange("p (t a) -> p t a", a=2), stats[:, k, :, :, 2],
                                            P * EPS, None, ALU.add).then_inc(s_var, 1)

                def mix(p, i, k, u):
                    dve.wait_ge(s_tanh, units(p, i, u))
                    nc.vector.scalar_tensor_tensor(out=th[:, k, cols(u)], in0=th[:, k, cols(u)], scalar=0.01,
                                                   in1=p_y[:, cols(u)], op0=ALU.mult,
                                                   op1=ALU.add).then_inc(s_u, 1)

                def finish(p, i, c):
                    for u in range(UNITS):
                        dve.wait_ge(s_back, results(p, i, u))
                        wait(dve, s_out[u], 16 * (p * FLIGHT + c))
                        tile = p * PT + c * CT + u * UT
                        nc.vector.tensor_tensor(out_sb[:, u].rearrange("p (t c) -> p t c", t=UT),
                                                p_back[:].rearrange("p (t c) -> p t c", t=UT),
                                                x_sb[:, bass.ds(tile, UT), :], ALU.add).then_inc(s_sum, 1)

                def body(p):
                    wait(dve, s_y, products(p, -FLIGHT, -1))
                    for t in range(0, PT, 2):
                        last = nc.vector.bn_stats(stats_x[:, t // 2].rearrange("p a s -> p (a s)"),
                                                  x_sb[:, bass.ds(p * PT + t, 2), :].rearrange("p a c -> p c a"))
                    last.then_inc(s_xchain, 1)
                    dve.wait_ge(s_xchain, p + 1)
                    nc.vector.tensor_scalar(var_x[:].rearrange("p (t a) -> p t a", a=2), stats_x[:, :, :, 2],
                                            1.0 / P, EPS, ALU.mult, ALU.add).then_inc(s_xvar, 1)
                    dve.wait_ge(s_xrstd, p + 1)
                    for t in range(PT):
                        last = nc.vector.tensor_scalar(xn[:, t, :], x_sb[:, p * PT + t, :], stats_x[:, t // 2, t % 2, 1:2],
                                                       rstd_x[:, t:t + 1], ALU.subtract, ALU.mult)
                        if t % UT == UT - 1:
                            last.then_inc(s_xn, 1)
                    for c in range(FLIGHT):
                        mix(p, c, c % 2, 0)
                        if c < FLIGHT - 1:
                            mix(p, c, c % 2, 1)
                    for i in range(2):
                        statistics(p, i, i)
                        variance(p, i, i)
                    with dve.Fori(0, ITERS - 1) as it:
                        for c in range(FLIGHT):
                            i = FLIGHT * it + c
                            scale_g(p, i, c, 0)
                            mix(p, i + FLIGHT - 1, 1 - c % 2, 1)
                            scale_g(p, i, c, 1)
                            statistics(p, i + 2, c % 2)
                            variance(p, i + 2, c % 2)
                            mix(p, i + FLIGHT, c % 2, 0)
                    for c in range(FLIGHT):
                        i = LAST + c
                        scale_g(p, i, c, 0)
                        if c == 0:
                            mix(p, i + FLIGHT - 1, 1, 1)
                        scale_g(p, i, c, 1)
                        if i + 2 < STEPS:
                            statistics(p, i + 2, c % 2)
                            variance(p, i + 2, c % 2)
                        finish(p, i, c)

                passes(dve, body)

            @block.tensor
            def _(pe):
                pe.wait_ge(s_prep, 4)
                nc.tensor.transpose(p_back[:, 0:P], w_centred[:], ident[:]).then_inc(s_prep_pe, 1)
                pe.wait_ge(s_prep, 8)
                pe.wait_ge(s_pick, 4)

                def transpose_g(p, i, c, first=False, some=range(UNITS)):
                    for u in some:
                        pe.wait_ge(s_g, units(p, i, u))
                        wait(pe, s_bn, units(p, -1) if first else units(p, i - 1, u))
                        for t in range(u * UT, (u + 1) * UT):
                            last = nc.tensor.transpose(p_gt[:, t * P:(t + 1) * P], g[:, c, t * P:(t + 1) * P], ident[:])
                        last.then_inc(s_gt, 1)

                def transpose_parts(p, i, k):
                    pe.wait_ge(s_parts, steps(p, i))
                    wait(pe, s_rts, steps(p, i) - 1)
                    nc.tensor.transpose(p_rt[:, k, :], parts[:, k].rearrange("p a t -> p (a t)"),
                                        ident_bf[:]).then_inc(s_rt, 1)

                def broadcast(p, i, k, first=False, some=range(UNITS)):
                    pe.wait_ge(s_rts, steps(p, i))
                    for u in some:
                        wait(pe, s_gs, units(p, -1) if first else units(p, i - 1, u))
                        for t in range(u * UT, (u + 1) * UT):
                            last = nc.tensor.matmul(p_rb[:, t * P:(t + 1) * P], pick[:, t, :], parts_t[:, k, :],
                                                    start=True, stop=True)
                        last.then_inc(s_rb, 1)

                def product(p, i, k, last_reader, some=range(UNITS)):
                    for u in some:
                        pe.wait_ge(s_gs, units(p, i, u))
                        pe.wait_ge(*last_reader(u))
                        nc.tensor.matmul(p_y[:, cols(u)], w_main[:], gs[:, k, cols(u)],
                                         start=True, stop=True).then_inc(s_y, 1)

                def body(p):
                    for c in range(FLIGHT):
                        for u in range(UNITS):
                            pe.wait_ge(s_xn, (p * FLIGHT + c) * UNITS + u + 1)
                            if c:
                                pe.wait_ge(s_u, units(p, c - 1, u))
                            else:
                                wait(pe, s_res, p * FLIGHT * UNITS)
                            for t in range(u * UT, (u + 1) * UT):
                                last = nc.tensor.transpose(p_y[:, t * P:(t + 1) * P], xn[:, c * CT + t, :], ident[:])
                            last.then_inc(s_y, 1)
                    for i in range(3):
                        transpose_g(p, i, i, first=(i == 0), some=range(UNITS) if i < 2 else [0])
                    transpose_parts(p, 0, 0)
                    broadcast(p, 0, 0, first=True)
                    with pe.Fori(0, ITERS - 1) as it:
                        for c in range(FLIGHT):
                            i = FLIGHT * it + c
                            k = c % 2
                            reader = lambda u: (s_u, units(p, i + FLIGHT - 1, u))
                            product(p, i, k, reader, [0])
                            transpose_g(p, i + 2, (c + 2) % FLIGHT, some=[1])
                            transpose_parts(p, i + 1, 1 - k)
                            product(p, i, k, reader, [1])
                            broadcast(p, i + 1, 1 - k)
                            transpose_g(p, i + 3, (c + 3) % FLIGHT, some=[0])
                    for c in range(FLIGHT):
                        i = LAST + c
                        k = c % 2
                        if c:
                            product(p, i, k, lambda u: (s_res, results(p, i - 1, u)))
                        else:
                            product(p, i, k, lambda u: (s_u, units(p, i + FLIGHT - 1, u)))
                        if i + 1 < STEPS:
                            transpose_parts(p, i + 1, 1 - k)
                        if i + 2 < STEPS:
                            transpose_g(p, i + 2, (c + 2) % FLIGHT, some=[1])
                        if i + 3 < STEPS:
                            transpose_g(p, i + 3, (c + 3) % FLIGHT, some=[0])
                        if i + 1 < STEPS:
                            broadcast(p, i + 1, 1 - k)
                        for u in range(UNITS):
                            pe.wait_ge(s_res, results(p, i, u))
                            wait(pe, s_sum, results(p, i, u) - 1)
                            for t in range(UT):
                                last = nc.tensor.transpose(p_back[:, t * P:(t + 1) * P],
                                                           res[:, u, t * P:(t + 1) * P], ident[:])
                            last.then_inc(s_back, 1)

                passes(pe, body)

            @block.scalar
            def _(act):
                def take_parts(p, i, k):
                    act.wait_ge(s_rt, steps(p, i))
                    wait(act, s_rb, units(p, i - 1))
                    nc.scalar.copy(parts_t[:, k, :], p_rt[:, k, :]).then_inc(s_rts, 1)

                def silu(p, i, c, b, some=range(UNITS)):
                    for u in some:
                        act.wait_ge(s_u, units(p, i, u))
                        nc.scalar.activation(g[:, c, cols(u)], th[:, c % 2, cols(u)], ACT.Silu,
                                             bias=b).then_inc(s_g, 1)

                def tanh(p, i, c, b, first=False, some=range(UNITS)):
                    for u in some:
                        act.wait_ge(s_y, products(p, i - FLIGHT, u))
                        wait(act, s_g, units(p, -1) if first else units(p, i - 2, u))
                        nc.scalar.activation(th[:, c % 2, cols(u)], p_y[:, cols(u)], ACT.Tanh,
                                             bias=b).then_inc(s_tanh, 1)

                act.wait_ge(s_prep, 7)
                def body(p):
                    for c in range(FLIGHT):
                        tanh(p, c, c, 0.0, first=(c < 2))
                        if c >= 1:
                            silu(p, c - 1, c - 1, 0.0)
                    silu(p, FLIGHT - 1, FLIGHT - 1, 0.0, [0])
                    take_parts(p, 0, 0)
                    silu(p, FLIGHT - 1, FLIGHT - 1, 0.0, [1])
                    with act.Fori(0, ITERS - 1) as it:
                        for c in range(FLIGHT):
                            i = FLIGHT * it + c
                            tanh(p, i + FLIGHT, c, bias[:], some=[0])
                            take_parts(p, i + 1, 1 - c % 2)
                            tanh(p, i + FLIGHT, c, bias[:], some=[1])
                            silu(p, i + FLIGHT, c, bias[:])
                    for c in range(FLIGHT):
                        i = LAST + c
                        for u in range(UNITS):
                            act.wait_ge(s_y, products(p, i, u))
                            wait(act, s_back, results(p, i - 1, u) if c else results(p, LAST, -1))
                            nc.scalar.activation(res[:, u, :], p_y[:, cols(u)], ACT.Identity,
                                                 bias=bias[:]).then_inc(s_res, 1)
                        if i + 1 < STEPS:
                            take_parts(p, i + 1, 1 - c % 2)

                passes(act, body)


def make_constants(nc, ident, ident_bf, minus_half):
    with nc.semaphore("constants") as s_const, nc.Block() as block:
        @block.gpsimd
        def _(pool):
            nc.gpsimd.memset(ident[:], 0.0).then_inc(s_const, 1)
            nc.gpsimd.memset(ident_bf[:], 0.0).then_inc(s_const, 1)
            nc.gpsimd.memset(minus_half[:], -0.5).then_inc(s_const, 1)
            pool.wait_ge(s_const, 3)
            for m in (ident, ident_bf):
                nc.gpsimd.affine_select(out=m[:], in_=m[:], compare_op=ALU.not_equal, fill=1.0, base=0,
                                        pattern=[[-1, P]], channel_multiplier=1).then_inc(s_const, 1)
            pool.wait_ge(s_const, 5)


def graph_transformer(nc, arg, out):
    n_graphs = arg["x"].shape[0]
    with ExitStack() as ctx:
        x_sb = ctx.enter_context(nc.sbuf_tensor("x_sb", [P, n_graphs, P], F32))
        ident = ctx.enter_context(nc.sbuf_tensor("ident", [P, P], F32))
        ident_bf = ctx.enter_context(nc.sbuf_tensor("ident_bf", [P, P], BF16))
        minus_half = ctx.enter_context(nc.sbuf_tensor("minus_half", [P, P], F32))
        env = dict(ident=ident, ident_bf=ident_bf, minus_half=minus_half)
        make_constants(nc, ident, ident_bf, minus_half)

        first = [arg["L0_gnn_" + name] for name in ("Wq", "Wk", "Wv", "Wo", "bq", "bk", "bv", "bo", "gamma", "beta")]
        graph_attention(nc, env, "a0_", x_sb, arg["adj"], first, heads=4, transposed=True, normed=True,
                        masked_op=ALU.is_equal, N_GRAPHS=n_graphs, x_in=arg["x"])
        mixture_ffn(nc, env, x_sb, *[arg["L0_ffn_" + name] for name in ("router_w", "w1", "b1", "w2", "b2")],
                    N_TILES=n_graphs)
        second = [arg["L1_gnn_" + name] for name in ("Wq", "Wk", "Wv", "Wo")] + [None] * 3 + [arg["L1_gnn_bo"], None, None]
        graph_attention(nc, env, "a1_", x_sb, arg["adj"], second, heads=8, transposed=False, normed=False,
                        masked_op=ALU.is_le, N_GRAPHS=n_graphs)
        recurrent_ffn(nc, env, x_sb, out, *[arg["L1_ffn_" + name] for name in ("ln_w", "ln_b", "W", "b")],
                      N_TILES=n_graphs)


_INS = ["x", "adj", "L0_gnn_Wq", "L0_gnn_bq", "L0_gnn_Wk", "L0_gnn_bk", "L0_gnn_Wv", "L0_gnn_bv", "L0_gnn_Wo",
        "L0_gnn_bo", "L0_gnn_gamma", "L0_gnn_beta", "L0_ffn_router_w", "L0_ffn_w1", "L0_ffn_b1", "L0_ffn_w2",
        "L0_ffn_b2", "L1_gnn_Wq", "L1_gnn_Wk", "L1_gnn_Wv", "L1_gnn_Wo", "L1_gnn_bo", "L1_ffn_ln_w",
        "L1_ffn_ln_b", "L1_ffn_W", "L1_ffn_b"]


def kernel(**inputs):
    import concourse.bacc as _bacc
    from concourse.bass_utils import run_bass_kernel_spmd as _run

    nc = _bacc.Bacc("TRN2", target_bir_lowering=False, num_devices=1)
    arrays, arg = {}, {}
    for name in _INS:
        a = np.ascontiguousarray(inputs[name])
        arrays[f"in_{name}_dram"] = a
        arg[name] = nc.dram_tensor(f"in_{name}_dram", a.shape, mybir.dt.from_np(a.dtype), kind="ExternalInput").ap()
    out = nc.dram_tensor("out_0_dram", inputs["x"].shape, F32, kind="ExternalOutput").ap()
    graph_transformer(nc, arg, out)
    r = _run(nc, [arrays], core_ids=[0])
    return r.results[0]["out_0_dram"]
```

```python
import numpy as np
from contextlib import ExitStack
from concourse import bass, mybir

F32 = mybir.dt.float32
BF16 = mybir.dt.bfloat16
I32 = mybir.dt.int32
F32R = mybir.dt.float32r
ALU = mybir.AluOpType
ACT = mybir.ActivationFunctionType
AX = mybir.AxisListType
P = 128
EPS = 1e-5
MASKED = -2.0 ** 100


def graph_attention(nc, env, tag, x_sb, adj, weights, heads, transposed, normed, masked_op, mask_on_vector,
                    N_GRAPHS=128, x_in=None):
    D = P // heads
    HU = 4
    UG = heads // HU
    QG = 4
    NU = QG * UG
    QUADS = N_GRAPHS // QG
    TOTAL = QUADS * NU
    SCALE = float(np.float32(D) ** np.float32(-0.5))
    Q_SCALE, EXP_SCALE = (1.0, SCALE) if np.log2(SCALE) % 1 == 0 else (SCALE, 1.0)
    assert normed or Q_SCALE == 1.0
    VW = D + 1
    QUAD = QG * P
    FIRST_KEYS = 0 if UG == 1 else 1
    KEY_SLOTS = NU - 2 - FIRST_KEYS
    NORM_SLOTS = (NU // 2, NU // 2) if UG == 1 else (NU - 3, NU - 2)

    with ExitStack() as ctx:
        sb = lambda n, s, d=F32: ctx.enter_context(nc.sbuf_tensor(tag + n, s, d))
        pb = lambda n, s, d=F32: ctx.enter_context(nc.psum_tensor(tag + n, s, d))
        sem = lambda n: ctx.enter_context(nc.semaphore(tag + n))
        ident, ident_bf, minus_half = env["ident"], env["ident_bf"], env["minus_half"]

        w_raw = sb("w_raw", [P, 4, P])
        w_q, w_k, w_v, w_o = (sb(f"w_{x}", [P, P]) for x in "qkvo")
        head_mask = sb("head_mask", [P, heads])
        cols_in = sb("cols_in", [P, 3])
        bv_bc = sb("bv_bc", [P, P])
        out_bias = sb("out_bias", [P, P])
        gamma = sb("gamma", [P, P])
        beta = sb("beta", [P, P])
        adj_in = sb("adj_in", [P, 2, QG, P], I32)
        mask = sb("mask", [P, 2, QG, P], BF16)
        stats = sb("stats", [P, QG // 2, 2, 3])
        var = sb("var", [P, QG])
        rstd = sb("rstd", [P, QG])
        xn = sb("xn", [P, QG, P])
        xn_t = sb("xn_t", [P, 2, QUAD])
        q_t = sb("q_t", [P, 2, QUAD])
        k_t = sb("k_t", [P, QUAD])
        k_heads = sb("k_heads", [P, 2, QG, heads, P])
        v_ones = sb("v_ones", [P, 2, QG, heads, VW])
        neg_max = sb("neg_max", [P, 2, HU])
        row_max = sb("row_max", [P, 2, HU])
        if mask_on_vector:
            masked = sb("masked", [P, 2, HU, P])
        prob = sb("prob", [P, 2, HU, P])
        prob_t = sb("prob_t", [P, 2, HU, P])
        rden = sb("rden", [P, HU])
        context = sb("context", [P, 2, P])
        context_t = sb("context_t", [P, 2, P])
        if normed:
            proj = sb("proj", [P, QG, P])
            stats_o = sb("stats_o", [P, QG // 2, 2, 3])
            var_o = sb("var_o", [P, QG])
            rstd_o = sb("rstd_o", [P, QG])
            proj_n = sb("proj_n", [P, QG, P])

        p_s = pb("p_s", [P, 2, HU, P])
        p_pt = pb("p_pt", [P, HU, P])
        p_pv = pb("p_pv", [P, HU, VW])
        p_ct = pb("p_ct", [P, P])
        p_o = pb("p_o", [P, QG, P])
        p_a = pb("p_a", [P, QUAD])
        p_b = pb("p_b", [P, QUAD])

        s_w = sem("weights_loaded")
        s_wt = sem("weight_transposed")
        s_prep = sem("prep_chain")
        s_hm = sem("head_mask_chain")
        pieces = [0, 1, 6, QUADS] if x_in is not None else [0]
        s_x = [sem(f"x_loaded_{i}") for i in range(len(pieces) - 1)]
        s_adj = [sem(f"adj_loaded_{i}") for i in range(2)]
        s_mask = sem("mask_ready")
        s_ln = sem("ln_chain")
        s_var = sem("var_ready")
        s_rstd = sem("rstd_ready")
        s_xn = sem("xn_ready")
        s_xt = sem("xn_transposed")
        s_xtc = sem("xn_t_ready")
        s_qmm = sem("q_product")
        s_kmm = sem("k_product")
        s_vmm = sem("v_product")
        s_q = sem("q_ready")
        s_kt = sem("k_taken")
        s_k = sem("k_ready")
        s_v = sem("v_ready")
        s_s = sem("scores_ready")
        s_masked = sem("masked_ready")
        s_max = sem("row_max_ready")
        s_neg = sem("neg_max_ready")
        s_exp = sem("prob_ready")
        s_tr = sem("prob_transposed")
        s_ptc = sem("prob_t_ready")
        s_pv = sem("context_product")
        s_rden = sem("rden_ready")
        s_norm = sem("context_ready")
        s_ct = sem("context_transposed")
        s_ctc = sem("context_t_ready")
        s_o = sem("projection_ready")
        s_fin = sem("projection_taken")
        s_fln = sem("out_ln_chain")
        s_fvar = sem("out_var_ready")
        s_frstd = sem("out_rstd_ready")
        s_fn = sem("out_normed")
        s_fp = sem("out_pool_chain")
        s_done = sem("x_updated")

        Wq, Wk, Wv, Wo, bq, bk, bv, bo, g_in, b_in = weights

        def live(q, limit):
            return not isinstance(q, int) or 0 <= q < limit

        def wait(eng, s, value):
            if not isinstance(value, int) or value > 0:
                eng.wait_ge(s, value)

        def quads(eng, body):
            for j in (-1, 0, 1):
                body(j, 0)
                body(j, 1)
            with eng.Fori(2, QUADS // 2 - 1) as j:
                body(j, 0)
                body(j, 1)
            for j in (QUADS // 2 - 1, QUADS // 2):
                body(j, 0)
                body(j, 1)

        scores_src = masked if mask_on_vector else p_s
        bank_read = s_masked if mask_on_vector else s_exp
        mask_used = s_masked if mask_on_vector else s_s

        def unit(k, u, ahead):
            return k + (u + ahead) // NU, (u + ahead) % NU

        adj_v = adj.rearrange("g n m -> n g m")
        row = lambda v: v.rearrange("(a c) -> a c", a=1).broadcast_to([P, P])
        col = lambda v: v.rearrange("(c a) -> c a", a=1)
        quad_row = lambda t: t[:].rearrange("p (a c) -> p a c", a=1).broadcast_to([P, QG, P])
        n_weights = 16 * (10 if normed else 5)
        n_prep = 7 if normed else 4

        with nc.Block() as block:
            @block.sync
            def _(sp):
                if x_in is not None:
                    x_v = x_in.rearrange("g n c -> n g c")
                    sp.dma_start(x_sb[:, 0:QG, :], x_v[:, 0:QG, :]).then_inc(s_x[0], 16)
                for j, w in enumerate((Wq, Wk, Wv, Wo)):
                    sp.dma_start(w_raw[:, j, :], w).then_inc(s_w, 16)
                if normed:
                    for j, v in enumerate((bq, bk, bv)):
                        sp.dma_start(cols_in[:, j:j + 1], col(v)).then_inc(s_w, 16)
                    sp.dma_start(gamma[:], row(g_in)).then_inc(s_w, 16)
                    sp.dma_start(beta[:], row(b_in)).then_inc(s_w, 16)
                sp.dma_start(out_bias[:], row(bo)).then_inc(s_w, 16)
                for k in range(2):
                    sp.dma_start(adj_in[:, k], adj_v[:, k * QG:(k + 1) * QG, :]).then_inc(s_adj[k], 16)
                if x_in is not None:
                    for i in range(1, len(s_x)):
                        part = slice(pieces[i] * QG, pieces[i + 1] * QG)
                        sp.dma_start(x_sb[:, part, :], x_v[:, part, :]).then_inc(s_x[i], 16)
                with sp.Fori(1, QUADS // 2) as j:
                    for par in range(2):
                        k = 2 * j + par
                        sp.wait_ge(s_mask, k - 1)
                        sp.dma_start(adj_in[:, par], adj_v[:, bass.ds(k * QG, QG), :]).then_inc(s_adj[par], 16)

            @block.gpsimd
            def _(pool):
                nc.gpsimd.memset(head_mask[:], 1.0).then_inc(s_hm, 1)
                nc.gpsimd.memset(v_ones[:], 1.0).then_inc(s_hm, 1)
                pool.wait_ge(s_hm, 2)
                nc.gpsimd.affine_select(out=head_mask[:], in_=head_mask[:], compare_op=ALU.is_ge, fill=0.0,
                                        base=0, pattern=[[-D, heads]], channel_multiplier=1).then_inc(s_hm, 1)
                pool.wait_ge(s_hm, 3)
                nc.gpsimd.affine_select(out=head_mask[:], in_=head_mask[:], compare_op=ALU.is_ge, fill=0.0,
                                        base=D - 1, pattern=[[D, heads]], channel_multiplier=-1).then_inc(s_hm, 1)
                pool.wait_ge(s_prep, n_prep)

                def body(j, par):
                    k = 2 * j + par
                    if live(k + 2, QUADS):
                        pool.wait_ge(s_var, k + 3)
                        nc.gpsimd.tensor_tensor(rstd[:], var[:], minus_half[:, 0:QG], ALU.pow).then_inc(s_rstd, 1)
                    if normed and live(k - 2, QUADS):
                        x_quad = x_sb[:, bass.ds((k - 2) * QG, QG), :]
                        pool.wait_ge(s_fn, k - 1)
                        nc.gpsimd.tensor_tensor(proj_n[:], proj_n[:], quad_row(gamma), ALU.mult).then_inc(s_fp, 1)
                        pool.wait_ge(s_fp, 2 * (k - 2) + 1)
                        nc.gpsimd.tensor_tensor(proj_n[:], proj_n[:], quad_row(beta), ALU.add).then_inc(s_fp, 1)
                        pool.wait_ge(s_fp, 2 * (k - 2) + 2)
                        nc.gpsimd.tensor_tensor(x_quad, x_quad, proj_n[:], ALU.add).then_inc(s_done, 1)
                    if live(k + 2, QUADS):
                        pool.wait_ge(s_adj[par], 16 * (j + 2))
                        wait(pool, mask_used, (k + 1) * NU)
                    if normed and live(k - 1, QUADS):
                        pool.wait_ge(s_fvar, k)
                        nc.gpsimd.tensor_tensor(rstd_o[:], var_o[:], minus_half[:, 0:QG], ALU.pow).then_inc(s_frstd, 1)
                    if not normed and live(k - 1, QUADS):
                        x_quad = x_sb[:, bass.ds((k - 1) * QG, QG), :]
                        pool.wait_ge(s_fin, k)
                        nc.gpsimd.tensor_tensor(x_quad, x_quad, quad_row(out_bias), ALU.add).then_inc(s_done, 1)
                    if live(k + 2, QUADS):
                        nc.gpsimd.tensor_scalar(mask[:, par], adj_in[:, par], 0.0, MASKED, masked_op,
                                                ALU.mult).then_inc(s_mask, 1)

                quads(pool, body)
                pool.wait_ge(s_done, QUADS)

            @block.vector
            def _(dve):
                chain = [0]

                def link(ins):
                    chain[0] += 1
                    ins.then_inc(s_prep, 1)
                    dve.wait_ge(s_prep, chain[0])

                dve.wait_ge(s_w, n_weights)
                for i, w in enumerate((w_q, w_k, w_v, w_o)):
                    if transposed:
                        dve.wait_ge(s_wt, 1)
                    link(nc.vector.tensor_copy(w[:], p_a[:, i * P:(i + 1) * P] if transposed else w_raw[:, i, :]))
                if normed:
                    link(nc.vector.tensor_copy(bv_bc[:], cols_in[:, 2:3].broadcast_to([P, P])))
                    dve.wait_ge(s_wt, 2)
                    link(nc.vector.tensor_tensor(out_bias[:], out_bias[:], p_b[:, 0:P], ALU.add))
                    link(nc.vector.tensor_scalar(cols_in[:, 0:1], cols_in[:, 0:1], Q_SCALE, None, ALU.mult))
                assert chain[0] == n_prep
                dve.wait_ge(s_hm, 4)

                def stats_x(k):
                    if x_in is not None:
                        piece = [i for i in range(len(s_x)) if isinstance(k, int) and pieces[i] <= k < pieces[i + 1]]
                        dve.wait_ge(s_x[piece[0] if piece else -1], 16)
                    wait(dve, s_xn, k)
                    for g in range(0, QG, 2):
                        last = nc.vector.bn_stats(stats[:, g // 2].rearrange("p a s -> p (a s)"),
                                                  x_sb[:, bass.ds(k * QG + g, 2), :].rearrange("p a c -> p c a"))
                    last.then_inc(s_ln, 1)
                    dve.wait_ge(s_ln, k + 1)
                    nc.vector.tensor_scalar(var[:].rearrange("p (g a) -> p g a", a=2), stats[:, :, :, 2],
                                            1.0 / P, EPS, ALU.mult, ALU.add).then_inc(s_var, 1)

                def normalise_x(k, half):
                    dve.wait_ge(s_rstd, k + 1)
                    wait(dve, s_xt, k)
                    for g in range(half * QG // 2, (half + 1) * QG // 2):
                        last = nc.vector.tensor_scalar(xn[:, g, :], x_sb[:, k * QG + g, :], stats[:, g // 2, g % 2, 1:2],
                                                       rstd[:, g:g + 1], ALU.subtract, ALU.mult)
                    if half:
                        last.then_inc(s_xn, 1)

                def keys(k, par, some):
                    if some[0] == 0:
                        dve.wait_ge(s_kt, k + 1)
                        wait(dve, s_s, (k - 1) * NU)
                    for h in some:
                        last = nc.vector.tensor_scalar(k_heads[:, par, :, h, :], k_t[:].rearrange("p (g m) -> p g m", g=QG),
                                                       head_mask[:, h:h + 1], None, ALU.mult)
                    if some[-1] == heads - 1:
                        last.then_inc(s_k, 1)

                def add_mask(k, par, u):
                    n, b, g = k * NU + u, u % 2, u // UG
                    dve.wait_ge(s_s, n + 1)
                    if u == 0:
                        dve.wait_ge(s_mask, k + 1)
                    wait(dve, s_exp, n - 1)
                    nc.vector.tensor_tensor(masked[:, b], p_s[:, b], mask[:, par, g:g + 1, :].broadcast_to([P, HU, P]),
                                            ALU.add).then_inc(s_masked, 1)

                def maximum(k, u):
                    n, b = k * NU + u, u % 2
                    dve.wait_ge(s_masked if mask_on_vector else s_s, n + 1)
                    nc.vector.tensor_reduce(out=row_max[:, b], in_=scores_src[:, b], axis=AX.X,
                                            op=ALU.max).then_inc(s_max, 1)

                def scale_maximum(k, u):
                    n, b = k * NU + u, u % 2
                    dve.wait_ge(s_max, n + 1)
                    wait(dve, s_exp, n - 1)
                    nc.vector.tensor_scalar(neg_max[:, b], row_max[:, b], -EXP_SCALE, None, ALU.mult).then_inc(s_neg, 1)

                def invert_sums(k, u):
                    dve.wait_ge(s_pv, k * NU + u + 1)
                    nc.vector.reciprocal(rden[:], p_pv[:, :, D]).then_inc(s_rden, 1)

                def normalise(k, u):
                    h0 = (u % UG) * HU
                    dve.wait_ge(s_rden, k * NU + u + 1)
                    if u % UG == 0:
                        wait(dve, s_ct, k * QG + u // UG - 1)
                    dst = context[:, u // UG % 2, h0 * D:(h0 + HU) * D]
                    nc.vector.tensor_tensor(dst.rearrange("p (h c) -> p h c", h=HU), p_pv[:, :, 0:D],
                                            rden[:].rearrange("p (h a) -> p h a", a=1).broadcast_to([P, HU, D]),
                                            ALU.mult).then_inc(s_norm, 1)

                def take_projection(k):
                    dve.wait_ge(s_o, (k + 1) * QG)
                    if not normed:
                        x_quad = x_sb[:, bass.ds(k * QG, QG), :]
                        nc.vector.tensor_tensor(x_quad, x_quad, p_o[:], ALU.add).then_inc(s_fin, 1)
                        return
                    wait(dve, s_fn, k)
                    nc.vector.tensor_tensor(proj[:], p_o[:], quad_row(out_bias), ALU.add).then_inc(s_fin, 1)
                    dve.wait_ge(s_fin, k + 1)
                    for g in range(0, QG, 2):
                        last = nc.vector.bn_stats(stats_o[:, g // 2].rearrange("p a s -> p (a s)"),
                                                  proj[:, g:g + 2, :].rearrange("p a c -> p c a"))
                    last.then_inc(s_fln, 1)
                    dve.wait_ge(s_fln, k + 1)
                    nc.vector.tensor_scalar(var_o[:].rearrange("p (g a) -> p g a", a=2), stats_o[:, :, :, 2],
                                            1.0 / P, EPS, ALU.mult, ALU.add).then_inc(s_fvar, 1)

                def normalise_projection(k):
                    dve.wait_ge(s_frstd, k + 1)
                    wait(dve, s_done, k)
                    for g in range(QG):
                        last = nc.vector.tensor_scalar(proj_n[:, g, :], proj[:, g, :], stats_o[:, g // 2, g % 2, 1:2],
                                                       rstd_o[:, g:g + 1], ALU.subtract, ALU.mult)
                    last.then_inc(s_fn, 1)

                def body(j, par):
                    k = 2 * j + par
                    for u in range(NU):
                        n = k * NU + u
                        if u == 3 and live(k - 1, QUADS):
                            take_projection(k - 1)
                        coming, passed = live(n + 2, TOTAL), live(n - 1, TOTAL)
                        some = [h for h in range(heads) if FIRST_KEYS + h * KEY_SLOTS // heads == u]
                        if not live(k + 1, QUADS):
                            some = []
                        if coming and mask_on_vector:
                            k2, u2 = unit(k, u, 2)
                            add_mask(k2, par if u2 >= 2 else 1 - par, u2)
                            if some:
                                keys(k + 1, 1 - par, some)
                                some = []
                        if coming:
                            maximum(*unit(k, u, 2))
                        if passed:
                            invert_sums(*unit(k, u, -1))
                        if coming:
                            scale_maximum(*unit(k, u, 2))
                        if passed:
                            normalise(*unit(k, u, -1))
                        if some:
                            keys(k + 1, 1 - par, some)
                        if u == 0 and live(k + 2, QUADS):
                            stats_x(k + 2)
                        if u == 1 and normed and live(k - 2, QUADS):
                            normalise_projection(k - 2)
                        for half in range(2):
                            if u == NORM_SLOTS[half] and live(k + 2, QUADS):
                                normalise_x(k + 2, half)

                quads(dve, body)

            @block.tensor
            def _(pe):
                pe.wait_ge(s_w, n_weights)
                if transposed:
                    for i in range(4):
                        last = nc.tensor.transpose(p_a[:, i * P:(i + 1) * P], w_raw[:, i, :], ident[:])
                    last.then_inc(s_wt, 1)
                    pe.wait_ge(s_prep, 5)
                    nc.tensor.matmul(p_b[:, 0:P], bv_bc[:], w_o[:], start=True, stop=True).then_inc(s_wt, 1)
                pe.wait_ge(s_prep, n_prep)

                def scores(k, par, u):
                    n, g, h0 = k * NU + u, u // UG, (u % UG) * HU
                    if u == 0:
                        if not mask_on_vector:
                            pe.wait_ge(s_mask, k + 1)
                        pe.wait_ge(s_q, k + 1)
                        pe.wait_ge(s_k, k + 1)
                    wait(pe, bank_read, n - 1)
                    if not mask_on_vector:
                        edges = mask[:, par, g:g + 1, :].broadcast_to([P, HU, P])
                        nc.tensor.matmul(p_s[:, u % 2], ident_bf[:], edges, start=True, stop=False)
                    nc.tensor.matmul(p_s[:, u % 2], q_t[:, par, g * P:(g + 1) * P], k_heads[:, par, g, h0:h0 + HU, :],
                                     start=mask_on_vector, stop=True).then_inc(s_s, 1)

                def transpose_prob(n, b):
                    pe.wait_ge(s_exp, n + 1)
                    wait(pe, s_ptc, n)
                    for h in range(HU):
                        last = nc.tensor.transpose(p_pt[:, h, :], prob[:, b, h, :], ident[:])
                    last.then_inc(s_tr, 1)

                def context_product(k, par, u):
                    n, g, h0 = k * NU + u, u // UG, (u % UG) * HU
                    if u == 0:
                        pe.wait_ge(s_v, k + 1)
                    pe.wait_ge(s_ptc, n + 1)
                    wait(pe, s_norm, n)
                    for h in range(HU):
                        last = nc.tensor.matmul(p_pv[:, h, :], prob_t[:, u % 2, h, :], v_ones[:, par, g, h0 + h, :],
                                                start=True, stop=True)
                    last.then_inc(s_pv, 1)

                def transpose_context(k, u):
                    graph = k * QG + u // UG
                    pe.wait_ge(s_norm, k * NU + u + 1)
                    wait(pe, s_ctc, graph)
                    nc.tensor.transpose(p_ct[:], context[:, u // UG % 2, :], ident[:]).then_inc(s_ct, 1)

                def project(k, u):
                    g = u // UG
                    pe.wait_ge(s_ctc, k * QG + g + 1)
                    if g == 0:
                        wait(pe, s_fin, k)
                    nc.tensor.matmul(p_o[:, g, :], context_t[:, g % 2, :], w_o[:], start=True, stop=True).then_inc(s_o, 1)

                def body(j, par):
                    k = 2 * j + par
                    for u in range(NU):
                        n = k * NU + u
                        if live(n + 2, TOTAL):
                            k2, u2 = unit(k, u, 2)
                            scores(k2, par if u2 >= 2 else 1 - par, u2)
                        if live(n, TOTAL):
                            transpose_prob(n, u % 2)
                        if live(n - 1, TOTAL):
                            k1, u1 = unit(k, u, -1)
                            context_product(k1, par if u else 1 - par, u1)
                        if live(n - 2, TOTAL) and (u - 2) % UG == UG - 1:
                            transpose_context(*unit(k, u, -2))
                        if live(n - 3, TOTAL) and (u - 3) % UG == UG - 1:
                            project(*unit(k, u, -3))
                        if u == 0 and live(k + 1, QUADS):
                            pe.wait_ge(s_xtc, k + 2)
                            wait(pe, s_v, k + 1)
                            nc.tensor.matmul(p_a[:], w_k[:], xn_t[:, 1 - par], start=True, stop=True).then_inc(s_kmm, 1)
                            nc.tensor.matmul(p_b[:], w_q[:], xn_t[:, 1 - par], start=True, stop=True).then_inc(s_qmm, 1)
                        if u == 1 and live(k + 1, QUADS):
                            pe.wait_ge(s_q, k + 2)
                            for g in range(QG):
                                last = nc.tensor.matmul(p_b[:, g * P:(g + 1) * P], xn_t[:, 1 - par, g * P:(g + 1) * P],
                                                        w_v[:], start=True, stop=True)
                            last.then_inc(s_vmm, 1)
                        if u == NU - 1 and live(k + 2, QUADS):
                            pe.wait_ge(s_xn, k + 3)
                            wait(pe, s_kt, k + 2)
                            for g in range(QG):
                                last = nc.tensor.transpose(p_a[:, g * P:(g + 1) * P], xn[:, g, :], ident[:])
                            last.then_inc(s_xt, 1)

                quads(pe, body)

            @block.scalar
            def _(act):
                act.wait_ge(s_hm, 2)
                act.wait_ge(s_prep, n_prep)

                def exponentials(k, u):
                    n = k * NU + u
                    act.wait_ge(s_neg, n + 1)
                    wait(act, s_tr, n - 1)
                    for h in range(HU):
                        last = nc.scalar.activation(prob[:, u % 2, h, :], scores_src[:, u % 2, h, :], ACT.Exp,
                                                    bias=neg_max[:, u % 2, h:h + 1], scale=EXP_SCALE)
                    last.then_inc(s_exp, 1)

                def body(j, par):
                    k = 2 * j + par
                    for u in range(NU):
                        n = k * NU + u
                        if live(n + 1, TOTAL):
                            exponentials(*unit(k, u, 1))
                        if live(n, TOTAL):
                            act.wait_ge(s_tr, n + 1)
                            wait(act, s_pv, n - 1)
                            nc.scalar.copy(prob_t[:, u % 2], p_pt[:]).then_inc(s_ptc, 1)
                        if live(n - 2, TOTAL) and (u - 2) % UG == UG - 1:
                            k2, u2 = unit(k, u, -2)
                            g = u2 // UG
                            act.wait_ge(s_ct, k2 * QG + g + 1)
                            wait(act, s_o, k2 * QG + g - 1)
                            nc.scalar.copy(context_t[:, g % 2, :], p_ct[:]).then_inc(s_ctc, 1)
                        if u == 0 and live(k + 1, QUADS):
                            act.wait_ge(s_kmm, k + 2)
                            wait(act, s_k, k + 1)
                            if normed:
                                nc.scalar.activation(k_t[:], p_a[:], ACT.Identity, bias=cols_in[:, 1:2]).then_inc(s_kt, 1)
                            else:
                                nc.scalar.copy(k_t[:], p_a[:]).then_inc(s_kt, 1)
                            act.wait_ge(s_qmm, k + 2)
                            wait(act, s_s, k * NU)
                            if normed:
                                nc.scalar.activation(q_t[:, 1 - par], p_b[:], ACT.Identity,
                                                     bias=cols_in[:, 0:1], scale=Q_SCALE).then_inc(s_q, 1)
                            else:
                                nc.scalar.copy(q_t[:, 1 - par], p_b[:]).then_inc(s_q, 1)
                        if u == 1 and live(k + 1, QUADS):
                            act.wait_ge(s_vmm, k + 2)
                            wait(act, s_pv, k * NU)
                            nc.scalar.copy(v_ones[:, 1 - par, :, :, 0:D],
                                           p_b[:].rearrange("p (g h c) -> p g h c", g=QG, h=heads)).then_inc(s_v, 1)
                        if u == NU - 1 and live(k + 2, QUADS):
                            act.wait_ge(s_xt, k + 3)
                            wait(act, s_vmm, k + 1)
                            nc.scalar.copy(xn_t[:, par], p_a[:]).then_inc(s_xtc, 1)

                quads(act, body)


def mixture_ffn(nc, env, x_sb, router_w, w1, b1, w2, b2, N_TILES=128):
    E = 8
    GT = 4
    GROUP = GT * P
    GROUPS = N_TILES // GT
    TOTAL = GROUPS * E
    GONE = -3.0e38

    with ExitStack() as ctx:
        sb = lambda n, s, d=F32: ctx.enter_context(nc.sbuf_tensor("m_" + n, s, d))
        pb = lambda n, s, d=F32: ctx.enter_context(nc.psum_tensor("m_" + n, s, d))
        sem = lambda n: ctx.enter_context(nc.semaphore("m_" + n))
        ident, minus_half = env["ident"], env["minus_half"]

        w1_sb = sb("w1_sb", [P, E, P])
        w1_hi = sb("w1_hi", [P, E, P], F32R)
        w1_lo = sb("w1_lo", [P, E, P], F32R)
        xt_hi = sb("xt_hi", [P, 2, GROUP], F32R)
        xt_lo = sb("xt_lo", [P, 2, GROUP], F32R)
        w2_sb = sb("w2_sb", [P, E, P])
        rows_in = sb("rows_in", [2 * E, P])
        cols = sb("cols", [P, 2, E])
        b2_blocks = sb("b2_blocks", [GT * E, GT, P])
        euler = sb("euler", [P, GT])
        index = sb("index", [P, GT, E])
        stats = sb("stats", [P, GT // 2, 2, 3])
        var = sb("var", [P, GT])
        rstd = sb("rstd", [P, GT])
        xn = sb("xn", [P, GT, P])
        xn_t = sb("xn_t", [P, 2, GROUP])
        hidden = sb("hidden", [P, 2, GROUP])
        logits = sb("logits", [P, GT, E])
        others = sb("others", [P, GT, E])
        same = sb("same", [P, GT, E])
        place = sb("place", [P, GT, E])
        first = sb("first", [P, GT, E])
        second = sb("second", [P, GT, E])
        top = sb("top", [P, 2, GT])
        where = sb("where", [P, 2, GT])
        gap = sb("gap", [P, GT])
        ratio = sb("ratio", [P, GT])
        total = sb("total", [P, GT])
        ones = sb("ones", [P, GT])
        minus_one = sb("minus_one", [P, GT])
        weighted = sb("weighted", [P, 2, GT, E])
        share = sb("share", [P, 2, GT])
        combine = sb("combine", [P, 2, GT, E])
        combine_t = sb("combine_t", [GT * E, P])

        p_h = pb("p_h", [P, 2, GROUP])
        p_y = pb("p_y", [P, 2, GT, P])
        p_xt = pb("p_xt", [P, GROUP])
        p_lg = pb("p_lg", [P, GT, E])
        p_ct = pb("p_ct", [GT * E, P])
        p_b2 = pb("p_b2", [P, GT, P])

        s_w = sem("weights_loaded")
        s_b2z = sem("b2_zeroed")
        s_const = sem("constants_ready")
        s_rt = sem("rows_transposed")
        s_cols = sem("cols_ready")
        s_ln = sem("ln_chain")
        s_var = sem("var_ready")
        s_rstd = sem("rstd_ready")
        s_xn = sem("xn_ready")
        s_xadd = sem("xn_added")
        s_xt = sem("xn_transposed")
        s_xtc = sem("xn_t_ready")
        s_w1 = sem("w1_split")
        s_lo = sem("xn_t_low_ready")
        s_lg = sem("logits_product")
        s_lgc = sem("logits_ready")
        s_route = sem("routing_chain")
        s_gap = sem("gap_ready")
        s_share = sem("share_chain")
        s_comb = sem("combine_ready")
        s_ct = sem("combine_transposed")
        s_ctc = sem("combine_t_ready")
        s_b2 = sem("b2_product")
        s_b2a = sem("b2_added")
        s_h = sem("hidden_product")
        s_gelu = sem("hidden_ready")
        s_y = sem("output_product")
        s_acc = sem("output_added")

        def live(q, limit):
            return not isinstance(q, int) or 0 <= q < limit

        def wait(eng, s, value):
            if not isinstance(value, int) or value > 0:
                eng.wait_ge(s, value)

        def groups(eng, body):
            body(-2, 0)
            body(-1, 1)
            body(0, 0)
            body(1, 1)
            with eng.Fori(1, GROUPS // 2 - 1) as j:
                body(2 * j, 0)
                body(2 * j + 1, 1)
            body(GROUPS - 2, 0)
            body(GROUPS - 1, 1)

        per_tile = lambda t: t.rearrange("p (g a) -> p g a", a=1).broadcast_to([P, GT, E])
        p_rows = p_lg[:].rearrange("p g e -> p (g e)")[:, 0:2 * E]
        ROUTE = 11

        with nc.Block() as block:
            @block.sync
            def _(sp):
                sp.dma_start(rows_in[0:E, :], router_w).then_inc(s_w, 16)
                sp.dma_start(rows_in[E:2 * E, :], b1).then_inc(s_w, 16)
                sp.dma_start(w1_sb[:], w1.rearrange("e c f -> c e f")).then_inc(s_w, 16)
                sp.dma_start(w2_sb[:], w2.rearrange("e f d -> f e d")).then_inc(s_w, 16)
                sp.wait_ge(s_b2z, 1)
                for t in range(GT):
                    sp.dma_start(b2_blocks[t * E:(t + 1) * E, t, :], b2).then_inc(s_w, 16)
                sp.wait_ge(s_w, 16 * 8)

            @block.gpsimd
            def _(pool):
                nc.gpsimd.memset(b2_blocks[:], 0.0).then_inc(s_b2z, 1)
                nc.gpsimd.memset(euler[:], float(np.e)).then_inc(s_const, 1)
                nc.gpsimd.memset(ones[:], 1.0).then_inc(s_const, 1)
                nc.gpsimd.memset(minus_one[:], -1.0).then_inc(s_const, 1)
                for e in range(E):
                    nc.gpsimd.memset(index[:, :, e], float(e - E)).then_inc(s_const, 1)
                pool.wait_ge(s_const, E + 3)

                def body(k, par):
                    if live(k + 2, GROUPS):
                        pool.wait_ge(s_var, k + 3)
                        nc.gpsimd.tensor_tensor(rstd[:], var[:], minus_half[:, 0:GT], ALU.pow).then_inc(s_rstd, 1)
                    if live(k + 1, GROUPS):
                        g = k + 1
                        pool.wait_ge(s_gap, g + 1)
                        nc.gpsimd.tensor_tensor(ratio[:], euler[:], gap[:], ALU.pow).then_inc(s_share, 1)
                        pool.wait_ge(s_share, 6 * g + 1)
                        nc.gpsimd.tensor_tensor(total[:], ratio[:], ones[:], ALU.add).then_inc(s_share, 1)
                        pool.wait_ge(s_share, 6 * g + 2)
                        nc.gpsimd.tensor_tensor(share[:, 0], total[:], minus_one[:], ALU.pow).then_inc(s_share, 1)
                        pool.wait_ge(s_share, 6 * g + 3)
                        nc.gpsimd.tensor_tensor(share[:, 1], ratio[:], share[:, 0], ALU.mult).then_inc(s_share, 1)
                        pool.wait_ge(s_share, 6 * g + 4)
                        pool.wait_ge(s_route, (g + 1) * ROUTE)
                        nc.gpsimd.tensor_tensor(weighted[:, 0], first[:], per_tile(share[:, 0]), ALU.mult).then_inc(s_share, 1)
                        nc.gpsimd.tensor_tensor(weighted[:, 1], second[:], per_tile(share[:, 1]), ALU.mult).then_inc(s_share, 1)
                        pool.wait_ge(s_share, 6 * g + 6)
                        wait(pool, s_acc, (g - 1) * E)
                        wait(pool, s_ct, g - 1)
                        nc.gpsimd.tensor_tensor(combine[:, 1 - par], weighted[:, 0], weighted[:, 1], ALU.add).then_inc(s_comb, 1)

                    if live(k + 2, GROUPS):
                        g = k + 2
                        x_group = x_sb[:, bass.ds(g * GT, GT), :]
                        pool.wait_ge(s_xn, g + 1)
                        nc.gpsimd.tensor_tensor(x_group, x_group, xn[:], ALU.add).then_inc(s_xadd, 1)

                groups(pool, body)

            @block.vector
            def _(dve):
                dve.wait_ge(s_rt, 1)
                nc.vector.tensor_copy(cols[:].rearrange("p a e -> p (a e)"), p_rows).then_inc(s_cols, 1)

                dve.wait_ge(s_w, 16 * 8)
                nc.vector.tensor_copy(w1_hi[:], w1_sb[:]).then_inc(s_w1, 1)
                dve.wait_ge(s_w1, 1)
                nc.vector.tensor_tensor(w1_lo[:], w1_sb[:], w1_hi[:], ALU.subtract).then_inc(s_w1, 1)
                dve.wait_ge(s_const, E + 3)

                def route(g, i):
                    done = g * ROUTE + i
                    if i == 0:
                        dve.wait_ge(s_lgc, g + 1)
                        wait(dve, s_comb, g)
                    elif i < ROUTE:
                        dve.wait_ge(s_route, done)
                    if i == 0:
                        op = nc.vector.tensor_reduce(out=top[:, 0], in_=logits[:], axis=AX.X, op=ALU.max)
                    elif i == 1:
                        op = nc.vector.tensor_tensor(same[:], logits[:], per_tile(top[:, 0]), ALU.is_equal)
                    elif i == 2:
                        op = nc.vector.tensor_tensor(place[:], same[:], index[:], ALU.mult)
                    elif i == 3:
                        op = nc.vector.tensor_reduce(out=where[:, 0], in_=place[:], axis=AX.X, op=ALU.min)
                    elif i == 4:
                        op = nc.vector.tensor_tensor(first[:], index[:], per_tile(where[:, 0]), ALU.is_equal)
                    elif i == 5:
                        op = nc.vector.scalar_tensor_tensor(out=others[:], in0=first[:], scalar=GONE, in1=logits[:],
                                                            op0=ALU.mult, op1=ALU.add)
                    elif i == 6:
                        op = nc.vector.tensor_reduce(out=top[:, 1], in_=others[:], axis=AX.X, op=ALU.max)
                    elif i == 7:
                        nc.vector.tensor_tensor(gap[:], top[:, 1], top[:, 0], ALU.subtract).then_inc(s_gap, 1)
                        op = nc.vector.tensor_tensor(same[:], others[:], per_tile(top[:, 1]), ALU.is_equal)
                    elif i == 8:
                        op = nc.vector.tensor_tensor(place[:], same[:], index[:], ALU.mult)
                    elif i == 9:
                        op = nc.vector.tensor_reduce(out=where[:, 1], in_=place[:], axis=AX.X, op=ALU.min)
                    elif i == 10:
                        op = nc.vector.tensor_tensor(second[:], index[:], per_tile(where[:, 1]), ALU.is_equal)
                    else:
                        return
                    op.then_inc(s_route, 1)

                def body(k, par):
                    for e in range(E):
                        n = k * E + e
                        if e == 0 and live(k + 2, GROUPS):
                            g = k + 2
                            wait(dve, s_xn, g)
                            for t in range(0, GT, 2):
                                last = nc.vector.bn_stats(stats[:, t // 2].rearrange("p a s -> p (a s)"),
                                                          x_sb[:, bass.ds(g * GT + t, 2), :].rearrange("p a c -> p c a"))
                            last.then_inc(s_ln, 1)
                            dve.wait_ge(s_ln, g + 1)
                            nc.vector.tensor_scalar(var[:].rearrange("p (t a) -> p t a", a=2), stats[:, :, :, 2],
                                                    1.0 / P, EPS, ALU.mult, ALU.add).then_inc(s_var, 1)
                        if e >= 6 and live(k + 2, GROUPS):
                            g = k + 2
                            dve.wait_ge(s_rstd, g + 1)
                            wait(dve, s_xt, g)
                            wait(dve, s_xadd, g)
                            for t in (range(0, GT // 2) if e == 6 else range(GT // 2, GT)):
                                last = nc.vector.tensor_scalar(xn[:, t, :], x_sb[:, g * GT + t, :], stats[:, t // 2, t % 2, 1:2],
                                                               rstd[:, t:t + 1], ALU.subtract, ALU.mult)
                            if e == 7:
                                last.then_inc(s_xn, 1)
                        if live(k, GROUPS):
                            if e == 0:
                                dve.wait_ge(s_comb, k + 1)
                                dve.wait_ge(s_xadd, k + 1)
                            dve.wait_ge(s_y, n + 1)
                            if e == 6:
                                dve.wait_ge(s_b2a, k + 1)
                            wait(dve, s_acc, n)
                        for t in range(GT):
                            if live(k, GROUPS):
                                x_tile = x_sb[:, k * GT + t, :]
                                last = nc.vector.scalar_tensor_tensor(out=x_tile, in0=p_y[:, e % 2, t, :],
                                                                      scalar=combine[:, par, t, e:e + 1], in1=x_tile,
                                                                      op0=ALU.mult, op1=ALU.add)
                                if t == GT - 1:
                                    last.then_inc(s_acc, 1)
                            if 2 <= e < 5 and live(k + 1, GROUPS):
                                route(k + 1, (e - 2) * GT + t)
                        if e == 1 and live(k + 1, GROUPS):
                            dve.wait_ge(s_xtc, k + 2)
                            wait(dve, s_h, k * E)
                            nc.vector.tensor_tensor(xt_lo[:, 1 - par, :], xn_t[:, 1 - par, :], xt_hi[:, 1 - par, :],
                                                    ALU.subtract).then_inc(s_lo, 1)
                        if e == 5 and live(k, GROUPS):
                            dve.wait_ge(s_b2, k + 1)
                            dve.wait_ge(s_acc, n + 1)
                            x_group = x_sb[:, bass.ds(k * GT, GT), :]
                            nc.vector.tensor_tensor(x_group, x_group, p_b2[:], ALU.add).then_inc(s_b2a, 1)

                groups(dve, body)

            @block.tensor
            def _(pe):
                pe.wait_ge(s_w, 16 * 8)
                nc.tensor.transpose(p_rows, rows_in[:], ident[0:2 * E, 0:2 * E]).then_inc(s_rt, 1)
                pe.wait_ge(s_cols, 1)
                pe.wait_ge(s_w1, 2)

                def hidden_product(k, par, e):
                    n = k * E + e
                    if e == 0:
                        pe.wait_ge(s_lo, k + 1)
                    wait(pe, s_gelu, n - 1)
                    nc.tensor.matmul(p_h[:, e % 2, :], w1_lo[:, e, :], xt_hi[:, par, :], start=True, stop=False)
                    nc.tensor.matmul(p_h[:, e % 2, :], w1_hi[:, e, :], xt_lo[:, par, :], start=False, stop=False)
                    nc.tensor.matmul(p_h[:, e % 2, :], w1_hi[:, e, :], xt_hi[:, par, :],
                                     start=False, stop=True).then_inc(s_h, 1)

                def output_product(k, e):
                    n = k * E + e
                    pe.wait_ge(s_gelu, n + 1)
                    wait(pe, s_acc, n - 1)
                    for t in range(GT):
                        last = nc.tensor.matmul(p_y[:, e % 2, t, :], hidden[:, e % 2, t * P:(t + 1) * P],
                                                w2_sb[:, e, :], start=True, stop=True)
                    last.then_inc(s_y, 1)

                def body(k, par):
                    g = k + 1
                    for e in range(E):
                        if e < E - 1:
                            if live(k, GROUPS):
                                hidden_product(k, par, e + 1)
                        elif live(g, GROUPS):
                            hidden_product(g, 1 - par, 0)
                        if live(k, GROUPS):
                            output_product(k, e)
                        if e == 0 and live(g, GROUPS):
                            pe.wait_ge(s_xn, g + 1)
                            wait(pe, s_xtc, g)
                            for t in range(GT):
                                last = nc.tensor.transpose(p_xt[:, t * P:(t + 1) * P], xn[:, t, :], ident[:])
                            last.then_inc(s_xt, 1)
                        if e == 1 and live(g, GROUPS):
                            pe.wait_ge(s_xtc, g + 1)
                            wait(pe, s_lgc, g)
                            for t in range(GT):
                                last = nc.tensor.matmul(p_lg[:, t, :], xn_t[:, 1 - par, t * P:(t + 1) * P], cols[:, 0, :],
                                                        start=True, stop=True)
                            last.then_inc(s_lg, 1)
                        if e == 1 and live(k, GROUPS):
                            pe.wait_ge(s_comb, k + 1)
                            wait(pe, s_ctc, k)
                            nc.tensor.transpose(p_ct[:], combine[:, par].rearrange("p g e -> p (g e)"),
                                                ident[:]).then_inc(s_ct, 1)
                        if e == 2 and live(k, GROUPS):
                            pe.wait_ge(s_ctc, k + 1)
                            wait(pe, s_b2a, k)
                            nc.tensor.matmul(p_b2[:], combine_t[:], b2_blocks[:], start=True, stop=True).then_inc(s_b2, 1)

                groups(pe, body)

            @block.scalar
            def _(act):
                act.wait_ge(s_cols, 1)

                def gelu(k, e):
                    n = k * E + e
                    act.wait_ge(s_h, n + 1)
                    wait(act, s_y, n - 1)
                    nc.scalar.activation(hidden[:, e % 2, :], p_h[:, e % 2, :], ACT.Gelu,
                                         bias=cols[:, 1, e:e + 1]).then_inc(s_gelu, 1)

                def body(k, par):
                    g = k + 1
                    for e in range(E):
                        if e < E - 1:
                            if live(k, GROUPS):
                                gelu(k, e + 1)
                        elif live(g, GROUPS):
                            gelu(g, 0)
                        if e == 0 and live(g, GROUPS):
                            act.wait_ge(s_xt, g + 1)
                            wait(act, s_h, (g - 1) * E)
                            wait(act, s_lg, g - 1)
                            wait(act, s_lo, g - 1)
                            nc.scalar.copy(xt_hi[:, 1 - par, :], p_xt[:])
                            nc.scalar.copy(xn_t[:, 1 - par, :], p_xt[:]).then_inc(s_xtc, 1)
                        if e == 1 and live(g, GROUPS):
                            act.wait_ge(s_lg, g + 1)
                            wait(act, s_comb, g)
                            nc.scalar.copy(logits[:], p_lg[:]).then_inc(s_lgc, 1)
                        if e == 1 and live(k, GROUPS):
                            act.wait_ge(s_ct, k + 1)
                            wait(act, s_b2, k)
                            nc.scalar.copy(combine_t[:], p_ct[:]).then_inc(s_ctc, 1)

                groups(act, body)


def recurrent_ffn(nc, env, x_sb, out_dram, ln_w, ln_b, w_dram, b_dram, N_TILES=128, ITERS=30):
    FLIGHT = 4
    CT = 8
    UT = 4
    UNITS = CT // UT
    CHUNK, UNIT = CT * P, UT * P
    PT = FLIGHT * CT
    PASSES = N_TILES // PT
    UNROLL = 3
    assert (ITERS - 3) % UNROLL == 0
    STEPS = ITERS * FLIGHT
    LAST = STEPS - FLIGHT

    with ExitStack() as ctx:
        sb = lambda n, s, d=F32: ctx.enter_context(nc.sbuf_tensor("d_" + n, s, d))
        pb = lambda n, s, d=F32: ctx.enter_context(nc.psum_tensor("d_" + n, s, d))
        sem = lambda n: ctx.enter_context(nc.semaphore("d_" + n))
        ident, ident_bf, minus_half = env["ident"], env["ident_bf"], env["minus_half"]

        w_rows = sb("w_rows", [P, P])
        w_centred = sb("w_centred", [P, P])
        w_main = sb("w_main", [P, P])
        lnw_bc = sb("lnw_bc", [P, P])
        lnb_bc = sb("lnb_bc", [P, P])
        row_sum = sb("row_sum", [P, 1])
        bias = sb("bias", [P, 1])
        b_col = sb("b_col", [P, 1])
        pick = sb("pick", [P, CT, P], BF16)
        xn = sb("xn", [P, PT, P])
        th = sb("th", [P, 2, CHUNK])
        g = sb("g", [P, FLIGHT, CHUNK])
        gs = sb("gs", [P, 2, CHUNK])
        stats = sb("stats", [P, 2, CT // 2, 2, 3])
        var = sb("var", [P, CT])
        rstd = sb("rstd", [P, CT])
        zeros = sb("zeros", [P, CT])
        epsilons = sb("epsilons", [P, CT])
        rem = sb("rem", [P, CT])
        parts = sb("parts", [P, 2, P // CT, CT], BF16)
        parts_t = sb("parts_t", [P, 2, P], BF16)
        stats_x = sb("stats_x", [P, FLIGHT, CT // 2, 2, 3])
        var_x = sb("var_x", [P, FLIGHT, CT])
        rstd_x = sb("rstd_x", [P, FLIGHT, CT])
        minus_mean = sb("minus_mean", [P, FLIGHT, CT])
        shift_x = sb("shift_x", [P, FLIGHT, CT])
        res = sb("res", [P, UNITS, UNIT])
        out_sb = sb("out_sb", [P, UNITS, UNIT])

        p_gt = pb("p_gt", [P, CHUNK])
        p_rb = pb("p_rb", [P, CHUNK])
        p_y = pb("p_y", [P, CHUNK])
        p_back = pb("p_back", [P, UNIT])
        p_rt = pb("p_rt", [P, 2, P], BF16)

        s_load = sem("weights_loaded")
        s_prep = sem("prep_chain")
        s_prep_pe = sem("prep_transposed")
        s_pick = sem("pick_chain")
        s_zero = sem("parts_zeroed")
        s_pool = sem("pool_chain")
        s_xchain = sem("x_chain")
        s_xvar = sem("x_var_ready")
        s_xpow = sem("x_rstd_chain")
        s_xrstd = sem("x_rstd_ready")
        s_xn = sem("xn_ready")
        s_xt = sem("xn_transposed")
        s_gt = sem("g_transposed")
        s_bn = sem("stats_ready")
        s_parts = sem("parts_ready")
        s_rt = sem("parts_transposed")
        s_rts = sem("parts_evacuated")
        s_rb = sem("rstd_broadcast")
        s_gs = sem("g_scaled")
        s_y = sem("product_ready")
        s_tanh = sem("tanh_ready")
        s_u = sem("u_ready")
        s_g = sem("g_ready")
        s_res = sem("result_evacuated")
        s_back = sem("result_transposed")
        s_sum = sem("result_summed")
        s_out = [sem(f"result_stored_{u}") for u in range(UNITS)]

        def steps(p, i):
            return p * STEPS + i + 1

        def units(p, i, u=UNITS - 1):
            return (p * STEPS + i) * UNITS + u + 1

        def products(p, i, u=UNITS - 1):
            return (p * STEPS + i + FLIGHT) * UNITS + u + 1

        def chunks(p, c):
            return p * FLIGHT + c + 1

        def x_transposes(p, c, u):
            return ((p - 1) * FLIGHT + c) * UNITS + u + 1

        def results(p, i, u=UNITS - 1):
            return (p * FLIGHT + i - LAST) * UNITS + u + 1

        def wait(eng, s, value):
            if not isinstance(value, int) or value > 0:
                eng.wait_ge(s, value)

        def passes(eng, body):
            body(0, True)
            with eng.Fori(1, PASSES - 1) as p:
                body(p, True)
            body(PASSES - 1, False)

        def iterations(eng, p, more, slot):
            for c in range(FLIGHT):
                slot(p, c, c, False)
            with eng.Fori(0, (ITERS - 3) // UNROLL) as it:
                for i in range(UNROLL * FLIGHT):
                    slot(p, FLIGHT * (UNROLL * it + 1) + i, i % FLIGHT, False)
            for c in range(FLIGHT):
                slot(p, LAST - FLIGHT + c, c, more)

        POOL_OPS = 5
        cols = lambda u: slice(u * UNIT, (u + 1) * UNIT)
        out_v = out_dram.rearrange("g n c -> n g c")

        with nc.Block() as block:
            @block.sync
            def _(sp):
                sp.dma_start(w_rows[:], w_dram).then_inc(s_load, 16)
                sp.dma_start(lnw_bc[:], ln_w.rearrange("(a c) -> a c", a=1).broadcast_to([P, P])).then_inc(s_load, 16)
                sp.dma_start(lnb_bc[:], ln_b.rearrange("(a c) -> a c", a=1).broadcast_to([P, P])).then_inc(s_load, 16)
                sp.dma_start(b_col[:], b_dram.rearrange("(c a) -> c a", a=1)).then_inc(s_load, 16)
                def body(p, more):
                    for i in range(LAST, STEPS):
                        for u in range(UNITS):
                            sp.wait_ge(s_sum, results(p, i, u))
                            tile = p * PT + (i - LAST) * CT + u * UT
                            sp.dma_start(out_v[:, bass.ds(tile, UT), :],
                                         out_sb[:, u].rearrange("p (t c) -> p t c", t=UT)).then_inc(s_out[u], 16)

                passes(sp, body)
                for u in range(UNITS):
                    sp.wait_ge(s_out[u], 16 * PASSES * FLIGHT)

            @block.gpsimd
            def _(pool):
                nc.gpsimd.memset(pick[:], 0.0).then_inc(s_pick, 1)
                nc.gpsimd.memset(parts[:], 0.0).then_inc(s_zero, 1)
                nc.gpsimd.memset(zeros[:], 0.0).then_inc(s_zero, 1)
                nc.gpsimd.memset(epsilons[:], P * EPS).then_inc(s_zero, 1)
                pool.wait_ge(s_zero, 3)
                for part in range(3):
                    pool.wait_ge(s_pick, part + 1)
                    nc.gpsimd.affine_select(out=pick[:], in_=pick[:], compare_op=ALU.not_equal, fill=1.0,
                                            base=-part * CT, pattern=[[-1, CT], [0, P]],
                                            channel_multiplier=1).then_inc(s_pick, 1)

                def step(p, i, k):
                    done = (p * STEPS + i) * POOL_OPS
                    pool.wait_ge(s_bn, units(p, i))
                    nc.gpsimd.tensor_tensor(var[:].rearrange("p (t a) -> p t a", a=2), stats[:, k, :, :, 2],
                                            epsilons[:].rearrange("p (t a) -> p t a", a=2), ALU.add).then_inc(s_pool, 1)
                    pool.wait_ge(s_pool, done + 1)
                    nc.gpsimd.tensor_tensor(rstd[:], var[:], minus_half[:, 0:CT], ALU.pow).then_inc(s_pool, 1)
                    pool.wait_ge(s_pool, done + 2)
                    wait(pool, s_rt, steps(p, i - 2))
                    nc.gpsimd.tensor_tensor(parts[:, k, 0], rstd[:], zeros[:], ALU.add).then_inc(s_pool, 1)
                    pool.wait_ge(s_pool, done + 3)
                    nc.gpsimd.tensor_tensor(parts[:, k, 1], rstd[:], parts[:, k, 0], ALU.subtract).then_inc(s_pool, 1)
                    nc.gpsimd.tensor_tensor(rem[:], rstd[:], parts[:, k, 0], ALU.subtract).then_inc(s_pool, 1)
                    pool.wait_ge(s_pool, done + 5)
                    nc.gpsimd.tensor_tensor(parts[:, k, 2], rem[:], parts[:, k, 1], ALU.subtract).then_inc(s_parts, 1)

                def rstd_of_x(p, c):
                    pool.wait_ge(s_xvar, chunks(p, c))
                    nc.gpsimd.tensor_tensor(rstd_x[:, c], var_x[:, c], minus_half[:, 0:CT], ALU.pow).then_inc(s_xpow, 1)
                    pool.wait_ge(s_xpow, chunks(p, c))
                    nc.gpsimd.tensor_tensor(shift_x[:, c], rstd_x[:, c], minus_mean[:, c], ALU.mult).then_inc(s_xrstd, 1)

                def slot(p, i, c, ahead):
                    step(p, i + 2, c % 2)
                    if ahead:
                        rstd_of_x(p + 1, c)

                def body(p, more):
                    iterations(pool, p, more, slot)
                    for c in range(FLIGHT if more else FLIGHT - 2):
                        step(p, LAST + c + 2, c % 2)

                for c in range(FLIGHT):
                    rstd_of_x(0, c)
                step(0, 0, 0)
                step(0, 1, 1)
                passes(pool, body)

            @block.vector
            def _(dve):
                chain = [0]

                def link(ins):
                    chain[0] += 1
                    ins.then_inc(s_prep, 1)
                    dve.wait_ge(s_prep, chain[0])

                dve.wait_ge(s_load, 64)
                link(nc.vector.tensor_tensor(w_centred[:], w_rows[:], lnw_bc[:], ALU.mult))
                link(nc.vector.tensor_reduce(out=row_sum[:], in_=w_centred[:], axis=AX.X, op=ALU.add))
                link(nc.vector.tensor_scalar(row_sum[:], row_sum[:], 1.0 / P, None, ALU.mult))
                link(nc.vector.tensor_scalar(w_centred[:], w_centred[:], row_sum[:], float(np.sqrt(P)),
                                             ALU.subtract, ALU.mult))
                link(nc.vector.tensor_tensor(lnb_bc[:], w_rows[:], lnb_bc[:], ALU.mult))
                link(nc.vector.tensor_reduce(out=bias[:], in_=lnb_bc[:], axis=AX.X, op=ALU.add))
                link(nc.vector.tensor_tensor(bias[:], bias[:], b_col[:], ALU.add))
                dve.wait_ge(s_prep_pe, 1)
                link(nc.vector.tensor_copy(w_main[:], p_back[:, 0:P]))

                def scale_g(p, i, c, u):
                    dve.wait_ge(s_rb, units(p, i, u))
                    dve.wait_ge(s_y, products(p, i - 2, u))
                    nc.vector.tensor_tensor(gs[:, c % 2, cols(u)], g[:, c, cols(u)], p_rb[:, cols(u)],
                                            ALU.mult).then_inc(s_gs, 1)

                def statistics(p, i, k):
                    wait(dve, s_parts, steps(p, i - 2))
                    for u in range(UNITS):
                        dve.wait_ge(s_gt, units(p, i, u))
                        for t in range(u * UT, (u + 1) * UT, 2):
                            last = nc.vector.bn_stats(stats[:, k, t // 2].rearrange("p a s -> p (a s)"),
                                                      p_gt[:, t * P:(t + 2) * P].rearrange("p (a c) -> p c a", a=2))
                        last.then_inc(s_bn, 1)

                def mix(p, i, k, u):
                    dve.wait_ge(s_tanh, units(p, i, u))
                    nc.vector.scalar_tensor_tensor(out=th[:, k, cols(u)], in0=th[:, k, cols(u)], scalar=0.01,
                                                   in1=p_y[:, cols(u)], op0=ALU.mult,
                                                   op1=ALU.add).then_inc(s_u, 1)

                def finish(p, i, c, u):
                    dve.wait_ge(s_back, results(p, i, u))
                    wait(dve, s_out[u], 16 * (p * FLIGHT + c))
                    tile = p * PT + c * CT + u * UT
                    nc.vector.tensor_tensor(out_sb[:, u].rearrange("p (t c) -> p t c", t=UT),
                                            p_back[:].rearrange("p (t c) -> p t c", t=UT),
                                            x_sb[:, bass.ds(tile, UT), :], ALU.add).then_inc(s_sum, 1)

                def stats_of_x(p, c, u):
                    wait(dve, s_xn, chunks(p - 1, c) * UNITS)
                    for t in range(u * UT, (u + 1) * UT, 2):
                        last = nc.vector.bn_stats(stats_x[:, c, t // 2].rearrange("p a s -> p (a s)"),
                                                  x_sb[:, bass.ds(p * PT + c * CT + t, 2), :].rearrange("p a c -> p c a"))
                    last.then_inc(s_xchain, 1)

                def variance_of_x(p, c):
                    dve.wait_ge(s_xchain, chunks(p, c) * UNITS)
                    nc.vector.tensor_scalar(minus_mean[:, c].rearrange("p (t a) -> p t a", a=2), stats_x[:, c, :, :, 1],
                                            -1.0, None, ALU.mult)
                    nc.vector.tensor_scalar(var_x[:, c].rearrange("p (t a) -> p t a", a=2), stats_x[:, c, :, :, 2],
                                            1.0 / P, EPS, ALU.mult, ALU.add).then_inc(s_xvar, 1)

                def slot(p, i, c, ahead):
                    scale_g(p, i, c, 0)
                    statistics(p, i + 2, c % 2)
                    mix(p, i + FLIGHT - 1, 1 - c % 2, 1)
                    if ahead:
                        stats_of_x(p + 1, c, 0)
                    scale_g(p, i, c, 1)
                    mix(p, i + FLIGHT, c % 2, 0)
                    if ahead:
                        stats_of_x(p + 1, c, 1)
                        variance_of_x(p + 1, c)

                def last_slot(p, i, c, more):
                    scale_g(p, i, c, 0)
                    if c:
                        finish(p, i - 1, c - 1, 1)
                    if more or i + 2 < STEPS:
                        statistics(p, i + 2, c % 2)
                    if more or c == 0:
                        mix(p, i + FLIGHT - 1, 1 - c % 2, 1)
                    scale_g(p, i, c, 1)
                    if more:
                        mix(p, i + FLIGHT, c % 2, 0)
                    finish(p, i, c, 0)
                    if c == FLIGHT - 1:
                        finish(p, i, c, 1)

                def body(p, more):
                    iterations(dve, p, more, slot)
                    for c in range(FLIGHT):
                        last_slot(p, LAST + c, c, more)

                for c in range(FLIGHT):
                    for u in range(UNITS):
                        stats_of_x(0, c, u)
                    variance_of_x(0, c)
                for c in range(FLIGHT):
                    mix(0, c, c % 2, 0)
                    if c < FLIGHT - 1:
                        mix(0, c, c % 2, 1)
                for i in range(2):
                    statistics(0, i, i)
                passes(dve, body)

            @block.tensor
            def _(pe):
                pe.wait_ge(s_prep, 4)
                nc.tensor.transpose(p_back[:, 0:P], w_centred[:], ident[:]).then_inc(s_prep_pe, 1)
                pe.wait_ge(s_prep, 8)
                pe.wait_ge(s_pick, 4)

                def transpose_g(p, i, c, u):
                    pe.wait_ge(s_g, units(p, i, u))
                    wait(pe, s_bn, units(p, i - 1, u))
                    for t in range(u * UT, (u + 1) * UT):
                        last = nc.tensor.transpose(p_gt[:, t * P:(t + 1) * P], g[:, c, t * P:(t + 1) * P], ident[:])
                    last.then_inc(s_gt, 1)

                def transpose_parts(p, i, k):
                    pe.wait_ge(s_parts, steps(p, i))
                    wait(pe, s_rts, steps(p, i) - 1)
                    nc.tensor.transpose(p_rt[:, k, :], parts[:, k].rearrange("p a t -> p (a t)"),
                                        ident_bf[:]).then_inc(s_rt, 1)

                def broadcast(p, i, k, u):
                    pe.wait_ge(s_rts, steps(p, i))
                    wait(pe, s_gs, units(p, i - 1, u))
                    for t in range(u * UT, (u + 1) * UT):
                        last = nc.tensor.matmul(p_rb[:, t * P:(t + 1) * P], pick[:, t, :], parts_t[:, k, :],
                                                start=True, stop=True)
                    last.then_inc(s_rb, 1)

                def product(p, i, k, u):
                    pe.wait_ge(s_gs, units(p, i, u))
                    nc.tensor.matmul(p_y[:, cols(u)], w_main[:], gs[:, k, cols(u)],
                                     start=True, stop=True).then_inc(s_y, 1)

                def transpose_x(c, u, signal):
                    for t in range(u * UT, (u + 1) * UT):
                        last = nc.tensor.transpose(p_y[:, t * P:(t + 1) * P], xn[:, c * CT + t, :], ident[:])
                    last.then_inc(signal, 1)

                def transpose_result(p, i, u):
                    pe.wait_ge(s_res, results(p, i, u))
                    wait(pe, s_sum, results(p, i, u) - 1)
                    for t in range(UT):
                        last = nc.tensor.transpose(p_back[:, t * P:(t + 1) * P],
                                                   res[:, u, t * P:(t + 1) * P], ident[:])
                    last.then_inc(s_back, 1)

                def slot(p, i, c, ahead):
                    k = c % 2
                    pe.wait_ge(s_u, units(p, i + FLIGHT - 1, 0))
                    product(p, i, k, 0)
                    transpose_parts(p, i + 1, 1 - k)
                    transpose_g(p, i + 3, (c + 3) % FLIGHT, 0)
                    broadcast(p, i + 1, 1 - k, 0)
                    pe.wait_ge(s_u, units(p, i + FLIGHT - 1, 1))
                    product(p, i, k, 1)
                    transpose_g(p, i + 3, (c + 3) % FLIGHT, 1)
                    broadcast(p, i + 1, 1 - k, 1)

                def last_slot(p, i, c, more):
                    k = c % 2
                    if more or c == 0:
                        pe.wait_ge(s_u, units(p, i + FLIGHT - 1, 0))
                    else:
                        pe.wait_ge(s_res, results(p, i - 1, 0))
                    product(p, i, k, 0)
                    if c:
                        transpose_result(p, i - 1, 1)
                    if more or i + 1 < STEPS:
                        transpose_parts(p, i + 1, 1 - k)
                    if more or i + 3 < STEPS:
                        transpose_g(p, i + 3, (c + 3) % FLIGHT, 0)
                    if more or i + 1 < STEPS:
                        broadcast(p, i + 1, 1 - k, 0)
                    if more:
                        pe.wait_ge(s_xn, chunks(p + 1, c) * UNITS - 1)
                        pe.wait_ge(s_res, results(p, i, 0))
                        transpose_x(c, 0, s_xt)
                    if more or c == 0:
                        pe.wait_ge(s_u, units(p, i + FLIGHT - 1, 1))
                    else:
                        pe.wait_ge(s_res, results(p, i - 1, 1))
                    product(p, i, k, 1)
                    transpose_result(p, i, 0)
                    if more:
                        pe.wait_ge(s_xn, chunks(p + 1, c) * UNITS)
                        pe.wait_ge(s_res, results(p, i, 1))
                        transpose_x(c, 1, s_xt)
                    if more or i + 3 < STEPS:
                        transpose_g(p, i + 3, (c + 3) % FLIGHT, 1)
                    if more or i + 1 < STEPS:
                        broadcast(p, i + 1, 1 - k, 1)
                    if c == FLIGHT - 1:
                        transpose_result(p, i, 1)

                def body(p, more):
                    iterations(pe, p, more, slot)
                    for c in range(FLIGHT):
                        last_slot(p, LAST + c, c, more)

                for c in range(FLIGHT):
                    for u in range(UNITS):
                        pe.wait_ge(s_xn, c * UNITS + u + 1)
                        wait(pe, s_u, units(0, c - 1, u))
                        transpose_x(c, u, s_y)
                for i in range(3):
                    for u in range(UNITS):
                        transpose_g(0, i, i, u)
                transpose_parts(0, 0, 0)
                for u in range(UNITS):
                    broadcast(0, 0, 0, u)
                passes(pe, body)

            @block.scalar
            def _(act):
                def take_parts(p, i, k):
                    act.wait_ge(s_rt, steps(p, i))
                    wait(act, s_rb, units(p, i - 1))
                    nc.scalar.copy(parts_t[:, k, :], p_rt[:, k, :]).then_inc(s_rts, 1)

                def silu(p, i, c, u, b):
                    act.wait_ge(s_u, units(p, i, u))
                    nc.scalar.activation(g[:, c, cols(u)], th[:, c % 2, cols(u)], ACT.Silu, bias=b).then_inc(s_g, 1)

                def tanh(p, i, c, u, b):
                    wait(act, s_g, units(p, i - 2, u))
                    nc.scalar.activation(th[:, c % 2, cols(u)], p_y[:, cols(u)], ACT.Tanh, bias=b).then_inc(s_tanh, 1)

                def normalise_x(p, c, u):
                    act.wait_ge(s_xrstd, chunks(p, c))
                    if not isinstance(p, int) or p > 1:
                        act.wait_ge(s_xt, x_transposes(p - 1, c, u))
                    elif p == 1:
                        act.wait_ge(s_y, products(0, c - FLIGHT, u))
                    for t in range(u * UT, (u + 1) * UT):
                        last = nc.scalar.activation(xn[:, c * CT + t, :], x_sb[:, p * PT + c * CT + t, :], ACT.Identity,
                                                    bias=shift_x[:, c, t:t + 1], scale=rstd_x[:, c, t:t + 1])
                    last.then_inc(s_xn, 1)

                def slot(p, i, c, ahead):
                    act.wait_ge(s_y, products(p, i, 0))
                    tanh(p, i + FLIGHT, c, 0, bias[:])
                    take_parts(p, i + 1, 1 - c % 2)
                    first = isinstance(i, int) and i == 0
                    silu(p, i + FLIGHT - 1, (c - 1) % FLIGHT, 1, 0.0 if first else bias[:])
                    if ahead and c:
                        normalise_x(p + 1, c - 1, 0)
                    act.wait_ge(s_y, products(p, i, 1))
                    tanh(p, i + FLIGHT, c, 1, bias[:])
                    silu(p, i + FLIGHT, c, 0, bias[:])
                    if ahead and c:
                        normalise_x(p + 1, c - 1, 1)

                def result(p, i, u):
                    act.wait_ge(s_y, products(p, i, u))
                    wait(act, s_back, results(p, i - 1, u) if i > LAST else results(p, LAST, -1))
                    nc.scalar.activation(res[:, u, :], p_y[:, cols(u)], ACT.Identity, bias=bias[:]).then_inc(s_res, 1)

                def last_slot(p, i, c, more):
                    result(p, i, 0)
                    if more or i + 1 < STEPS:
                        take_parts(p, i + 1, 1 - c % 2)
                    if more:
                        act.wait_ge(s_xt, x_transposes(p + 1, c, 0))
                        tanh(p, i + FLIGHT, c, 0, 0.0)
                    if more or c == 0:
                        silu(p, i + FLIGHT - 1, (c - 1) % FLIGHT, 1, 0.0 if c else bias[:])
                    result(p, i, 1)
                    if more:
                        act.wait_ge(s_xt, x_transposes(p + 1, c, 1))
                        tanh(p, i + FLIGHT, c, 1, 0.0)
                        silu(p, i + FLIGHT, c, 0, 0.0)
                        if c < UNITS:
                            normalise_x(p + 1, FLIGHT - 1, c)

                def body(p, more):
                    iterations(act, p, more, slot)
                    for c in range(FLIGHT):
                        last_slot(p, LAST + c, c, more)

                for u in range(UNITS):
                    normalise_x(0, 0, u)
                act.wait_ge(s_prep, 7)
                for c in range(FLIGHT):
                    for u in range(UNITS):
                        if c < FLIGHT - 1:
                            normalise_x(0, c + 1, u)
                        act.wait_ge(s_y, products(0, c - FLIGHT, u))
                        tanh(0, c, c, u, 0.0)
                    if c >= 1:
                        silu(0, c - 1, c - 1, 0, 0.0)
                        silu(0, c - 1, c - 1, 1, 0.0)
                silu(0, FLIGHT - 1, FLIGHT - 1, 0, 0.0)
                take_parts(0, 0, 0)
                passes(act, body)


def make_constants(nc, ident, ident_bf, minus_half):
    with nc.semaphore("constants") as s_const, nc.Block() as block:
        @block.gpsimd
        def _(pool):
            nc.gpsimd.memset(ident[:], 0.0).then_inc(s_const, 1)
            nc.gpsimd.memset(ident_bf[:], 0.0).then_inc(s_const, 1)
            nc.gpsimd.memset(minus_half[:], -0.5).then_inc(s_const, 1)
            pool.wait_ge(s_const, 3)
            for m in (ident, ident_bf):
                nc.gpsimd.affine_select(out=m[:], in_=m[:], compare_op=ALU.not_equal, fill=1.0, base=0,
                                        pattern=[[-1, P]], channel_multiplier=1).then_inc(s_const, 1)
            pool.wait_ge(s_const, 5)


def graph_transformer(nc, arg, out):
    n_graphs = arg["x"].shape[0]
    with ExitStack() as ctx:
        x_sb = ctx.enter_context(nc.sbuf_tensor("x_sb", [P, n_graphs, P], F32))
        ident = ctx.enter_context(nc.sbuf_tensor("ident", [P, P], F32))
        ident_bf = ctx.enter_context(nc.sbuf_tensor("ident_bf", [P, P], BF16))
        minus_half = ctx.enter_context(nc.sbuf_tensor("minus_half", [P, P], F32))
        env = dict(ident=ident, ident_bf=ident_bf, minus_half=minus_half)
        make_constants(nc, ident, ident_bf, minus_half)

        first = [arg["L0_gnn_" + name] for name in ("Wq", "Wk", "Wv", "Wo", "bq", "bk", "bv", "bo", "gamma", "beta")]
        graph_attention(nc, env, "a0_", x_sb, arg["adj"], first, heads=4, transposed=True, normed=True,
                        masked_op=ALU.is_equal, mask_on_vector=False, N_GRAPHS=n_graphs, x_in=arg["x"])
        mixture_ffn(nc, env, x_sb, *[arg["L0_ffn_" + name] for name in ("router_w", "w1", "b1", "w2", "b2")],
                    N_TILES=n_graphs)
        second = [arg["L1_gnn_" + name] for name in ("Wq", "Wk", "Wv", "Wo")] + [None] * 3 + [arg["L1_gnn_bo"], None, None]
        graph_attention(nc, env, "a1_", x_sb, arg["adj"], second, heads=8, transposed=False, normed=False,
                        masked_op=ALU.is_le, mask_on_vector=True, N_GRAPHS=n_graphs)
        recurrent_ffn(nc, env, x_sb, out, *[arg["L1_ffn_" + name] for name in ("ln_w", "ln_b", "W", "b")],
                      N_TILES=n_graphs)


_INS = ["x", "adj", "L0_gnn_Wq", "L0_gnn_bq", "L0_gnn_Wk", "L0_gnn_bk", "L0_gnn_Wv", "L0_gnn_bv", "L0_gnn_Wo",
        "L0_gnn_bo", "L0_gnn_gamma", "L0_gnn_beta", "L0_ffn_router_w", "L0_ffn_w1", "L0_ffn_b1", "L0_ffn_w2",
        "L0_ffn_b2", "L1_gnn_Wq", "L1_gnn_Wk", "L1_gnn_Wv", "L1_gnn_Wo", "L1_gnn_bo", "L1_ffn_ln_w",
        "L1_ffn_ln_b", "L1_ffn_W", "L1_ffn_b"]


def kernel(**inputs):
    import concourse.bacc as _bacc
    from concourse.bass_utils import run_bass_kernel_spmd as _run

    nc = _bacc.Bacc("TRN2", target_bir_lowering=False, num_devices=1)
    arrays, arg = {}, {}
    for name in _INS:
        a = np.ascontiguousarray(inputs[name])
        arrays[f"in_{name}_dram"] = a
        arg[name] = nc.dram_tensor(f"in_{name}_dram", a.shape, mybir.dt.from_np(a.dtype), kind="ExternalInput").ap()
    out = nc.dram_tensor("out_0_dram", inputs["x"].shape, F32, kind="ExternalOutput").ap()
    graph_transformer(nc, arg, out)
    r = _run(nc, [arrays], core_ids=[0])
    return r.results[0]["out_0_dram"]
```
